# Optimizing a Trainium2 kernel written in Bass

```python
import numpy as np
import jax
import jax.numpy as jnp

def _softmax(x, axis=-1):
    return jax.nn.softmax(x, axis=axis)

def _gelu(x):
    return jax.nn.gelu(x, approximate=True)

def _silu(x):
    return jax.nn.silu(x)

def _sigmoid(x):
    return jax.nn.sigmoid(x)

def _layernorm(x, axis=-1, eps=1e-05):
    m = jnp.mean(x, axis=axis, keepdims=True)
    v = jnp.var(x, axis=axis, keepdims=True)
    return (x - m) / jnp.sqrt(v + eps)

def _scatter_add(tgt, idx, src, axis=0):
    return tgt.at[idx].add(src)

def _segment_sum(src, seg, n):
    return jax.ops.segment_sum(src, seg, n)
kernel_name = 'mk_gnn_resnorm_d1_gnn_r8_c74cbb'

def setup_inputs(seed: int=0):
    np.random.seed(seed)
    _w = jnp.asarray

    def _rec_inputs():
        import jax
        import jax.numpy as jnp
        _gk = jax.random.key(seed)
        x = -0.0003713 + 1 * jax.random.normal(jax.random.fold_in(_gk, 1), (6250, 256), jnp.float32)
        src = jax.random.randint(jax.random.fold_in(_gk, 2), (100000,), 0, 6250, jnp.int32)
        dst = jnp.minimum((6250 * jax.random.uniform(jax.random.fold_in(_gk, 3), (100000,)) ** 2.0).astype(jnp.int32), 49999)
        _o = jnp.argsort(dst, stable=True)
        src = src[_o]
        dst = dst[_o]
        edge_attr_64 = 0.000189758 + 1.00013 * jax.random.normal(jax.random.fold_in(_gk, 12), (100000, 64), jnp.float32)
        return (x, src, dst, edge_attr_64)
    x, src, dst, edge_attr_64 = _rec_inputs()

    def _L0_gnn_setup():
        import jax, jax.numpy as jnp
        import numpy as np
        N_NODES = 6250
        N_EDGES = 100000
        NODE_IN = 256
        EDGE_OUT = 64
        GLOBAL_IN = 128
        NODE_OUT = 256
        HIDDEN = 512
        N_GRAPHS = 64
        key = jax.random.key(seed)
        ks = jax.random.split(key, 8)
        x = jax.random.normal(ks[0], (N_NODES, NODE_IN), dtype=jnp.float32)
        edge_index = jax.random.randint(ks[1], (2, N_EDGES), 0, N_NODES, dtype=jnp.int64)
        edge_attr = jax.random.normal(ks[2], (N_EDGES, EDGE_OUT), dtype=jnp.float32)
        u = jax.random.normal(ks[3], (N_GRAPHS, GLOBAL_IN), dtype=jnp.float32)
        batch = jnp.sort(jax.random.randint(ks[4], (N_NODES,), 0, N_GRAPHS, dtype=jnp.int64))
        in_dim = NODE_IN + EDGE_OUT + GLOBAL_IN
        b1s = 1.0 / np.sqrt(in_dim)
        b2s = 1.0 / np.sqrt(HIDDEN)
        W1 = jax.random.uniform(ks[5], (in_dim, HIDDEN), dtype=jnp.float32, minval=-b1s, maxval=b1s)
        b1 = jnp.zeros((HIDDEN,), dtype=jnp.float32)
        W2 = jax.random.uniform(ks[6], (HIDDEN, NODE_OUT), dtype=jnp.float32, minval=-b2s, maxval=b2s)
        b2 = jnp.zeros((NODE_OUT,), dtype=jnp.float32)
        return {'x': x, 'edge_index': edge_index, 'edge_attr': edge_attr, 'u': u, 'batch': batch, 'W1': W1, 'b1': b1, 'W2': W2, 'b2': b2}
    _L0_gnn_all = _L0_gnn_setup()
    _L0_gnn_in = {k: v for k, v in _L0_gnn_all.items() if k in ('u', 'W1', 'b1', 'W2', 'b2')}
    del _L0_gnn_all
    return {'x': x, 'src': src, 'dst': dst, 'edge_attr_64': edge_attr_64, 'L0_gnn_u': _L0_gnn_in['u'], 'L0_gnn_W1': _L0_gnn_in['W1'], 'L0_gnn_b1': _L0_gnn_in['b1'], 'L0_gnn_W2': _L0_gnn_in['W2'], 'L0_gnn_b2': _L0_gnn_in['b2']}

def reference(x, src, dst, edge_attr_64, L0_gnn_u, L0_gnn_W1, L0_gnn_b1, L0_gnn_W2, L0_gnn_b2):
    import jax
    import jax.numpy as jnp

    def _L0_gnn_ref(x, edge_index, edge_attr, u, batch, W1, b1, W2, b2):
        import jax, jax.numpy as jnp
        import numpy as np
        N_NODES = 6250
        N_EDGES = 100000
        NODE_IN = 256
        EDGE_OUT = 64
        GLOBAL_IN = 128
        NODE_OUT = 256
        HIDDEN = 512
        N_GRAPHS = 64
        n = x.shape[0]
        src = edge_index[0]
        sums = jax.ops.segment_sum(edge_attr, src, num_segments=n)
        counts = jax.ops.segment_sum(jnp.ones((edge_attr.shape[0],), edge_attr.dtype), src, num_segments=n)
        edge_attr_agg = sums / jnp.maximum(counts, 1.0)[:, None]
        u_expanded = u[batch]
        combined = jnp.concatenate([x, edge_attr_agg, u_expanded], axis=1)
        h = jax.nn.relu(combined @ W1 + b1)
        return h @ W2 + b2
    edge_index = jnp.stack([src, dst])
    batch0 = jnp.zeros((6250,), jnp.int32)
    x = _layernorm(x + _L0_gnn_ref(x, edge_index, edge_attr_64, L0_gnn_u, batch0, L0_gnn_W1, L0_gnn_b1, L0_gnn_W2, L0_gnn_b2), axis=-1)
    return x

_drawn_inputs = setup_inputs


def setup_inputs(seed=0):
    import zlib

    import numpy as np

    out = dict(_drawn_inputs(seed))
    spreads = {'L0_gnn_b1': (0.0, 0.1), 'L0_gnn_b2': (0.0, 0.1)}
    factors = {}
    for name, (base, spread) in spreads.items():
        noise = np.random.default_rng([zlib.crc32(name.encode()), seed]).standard_normal(out[name].shape)
        drawn = base * np.exp(spread * noise) if base else spread * noise
        out[name] = jnp.asarray(drawn.astype(out[name].dtype))
    for name, factor in factors.items():
        out[name] = (out[name] * factor).astype(out[name].dtype)
    return out
```

```python
from contextlib import ExitStack

import concourse.bass as bass
from concourse import mybir

F32 = mybir.dt.float32
I32 = mybir.dt.int32
U32 = mybir.dt.uint32
ALU = mybir.AluOpType
ACT = mybir.ActivationFunctionType
AX = mybir.AxisListType

P = 128
NODES, DIM = 6250, 256
EDGES, FEAT = 100000, 64
HID = 512
EPS = 1e-5

ROW = FEAT + 1
TILES = 5
UNITS = 4
TURNS = EDGES // (P * TILES * UNITS)
MAIN_COLS = TURNS * UNITS * TILES
MAIN_EDGES = MAIN_COLS * P
LAST_TILES = -(-(EDGES - MAIN_EDGES) // P)
LAST_ROWS = EDGES - MAIN_EDGES - (LAST_TILES - 1) * P
SRC_COLS = MAIN_COLS + LAST_TILES
ALL_UNITS = TURNS * UNITS + 1
FINAL_ORDER = [*range(LAST_TILES, TILES), *range(LAST_TILES)]
DUP = 256.0

NP = 125
COLS = NODES // NP
TABLE_ROWS = P * COLS
XPART = 112
KX = DIM // P
KH = HID // P
DENSE_TURNS = COLS // 2
PLAIN_TURNS = TURNS - DENSE_TURNS
X_PIECES = 10
X_PIECE = COLS * DIM // X_PIECES
assert X_PIECES < PLAIN_TURNS
CHUNKS = 5
CC = COLS // CHUNKS
CHUNK_STEPS = CC // 2
STEPS = COLS // 2
PAIR = 2 * CHUNK_STEPS
PAIRS = STEPS // PAIR
CHUNK_ROW = CC * ROW
NW = 2 * NP

ROWS_SLOTS = 2
SUM_SLOTS = 2
OUT_SLOTS = 4


def build(nc, x, src, attr, u, w1, b1, w2, b2, out):
    tables = [nc.dram_tensor(f"table{j}", [TABLE_ROWS, ROW], F32, kind="Internal").ap()
              for j in range(TILES)]
    src_main = src[0:MAIN_EDGES].rearrange("(p t) -> p t", p=P)
    attr_main = attr[0:MAIN_EDGES, :].rearrange("(p t) f -> p (t f)", p=P)
    x_v = x.rearrange("(p c) d -> p (c d)", p=NP)
    out_v = out.rearrange("(p c) d -> p (c d)", p=NP)
    table_v = [t.rearrange("(p c) r -> p (c r)", p=P) for t in tables]

    ctx = ExitStack()
    with ctx:
        def sb(name, shape, dt=F32):
            return ctx.enter_context(nc.sbuf_tensor(name, shape, dt))

        def pb(name, shape, dt=F32):
            return ctx.enter_context(nc.psum_tensor(name, shape, dt))

        def sem(name):
            return ctx.enter_context(nc.semaphore(name))

        ident = sb("ident", [P, P])
        same_weight = sb("same_weight", [P, P])
        spare_row = sb("spare_row", [P, 1])
        spare_i = sb("spare_i", [P, 1], I32)
        w1x = sb("w1x", [P, KX, HID])
        w1e = sb("w1e", [FEAT, HID])
        w2s = sb("w2s", [P, KH, DIM])
        b2_all = sb("b2_all", [P, DIM])
        b1_col = sb("b1_col", [P, KH])
        u_col = sb("u_col", [P, 1])
        hid_bias = sb("hid_bias", [P, KH])

        xs = sb("xs", [P, COLS * DIM])
        pre = sb("pre", [P, COLS * HID // P * NP])
        x_stage = [sb(f"x_stage{q}", [P, DIM]) for q in range(2)]
        xt = sb("xt", [P, KX, NP])
        partial = sb("partial", [P, TILES * CHUNK_ROW])
        rcount = sb("rcount", [P, CC])
        stats = sb("stats", [P, 2, 2, 6])
        mv = sb("mv", [P, 2, 2, 2])
        std = sb("std", [P, 2, 2])
        rstd = sb("rstd", [P, 2, 2])
        shift = sb("shift", [P, 2, 2])
        eps_col = sb("eps_col", [P, 1])

        srcf = sb("srcf", [P, SRC_COLS])
        src_unit = [sb(f"src_unit{s}", [P, TILES]) for s in range(UNITS)]
        t_dup = sb("t_dup", [P, TILES])
        idx = [sb(f"idx{s}", [P, TILES], U32) for s in range(UNITS)]
        A_ATTR, A_SAME = 0, 2 * TILES * FEAT * 2
        A_WSAME = A_SAME + 2 * TILES * P
        A_PAY = A_WSAME + TILES * P
        A_END = A_PAY + UNITS * TILES * ROW
        area = sb("area", [P, A_END])
        attr_s = [area[:, A_ATTR + a * 2 * TILES * FEAT:A_ATTR + (a + 1) * 2 * TILES * FEAT] for a in range(2)]
        same = [area[:, A_SAME + b * TILES * P:A_SAME + (b + 1) * TILES * P].rearrange("p (t e) -> p t e", e=P)
                for b in range(2)]
        wsame = area[:, A_WSAME:A_PAY].rearrange("p (t e) -> p t e", e=P)
        payload = [area[:, A_PAY + s * TILES * ROW:A_PAY + (s + 1) * TILES * ROW].rearrange("p (t r) -> p t r", r=ROW)
                   for s in range(UNITS)]
        at = 0
        node_area = []
        for length in (KH * NW, 2 * DIM, NW, CHUNK_ROW // 2):
            node_area.append([area[:, at + b * length:at + (b + 1) * length] for b in range(2)])
            at += 2 * length
        h_s, z, aggt, _ = node_area
        acc = [sb("acc0", [P, CHUNK_ROW])[:, :], area[:, at - CHUNK_ROW:at]]
        assert at <= A_END
        src_i = pre[:, 0:SRC_COLS].bitcast(I32)
        w1u = pre[:, 1024:1024 + HID]

        ps = pb("ps", [P, 8 * 512])
        rows_p = [ps[:, b * TILES * P:(b + 1) * TILES * P] for b in range(2)]
        sums_p = [ps[:, (3 + b) * 512:(3 + b) * 512 + TILES * FEAT] for b in range(2)]
        xt_p = ps[:, 5 * 512:5 * 512 + KX * NP]
        pre_p = ps[:, 6 * 512:6 * 512 + KH * NP]
        bias_p = ps[:, 7 * 512:7 * 512 + KH]
        h_p = [ps[:, 2 * b * 512:(2 * b + 2) * 512] for b in range(2)]
        y_p = [ps[:, (4 + b) * 512:(5 + b) * 512] for b in range(2)]
        aggt_p = [ps[0:FEAT, (6 + b) * 512:(6 + b) * 512 + NW] for b in range(2)]

        s_fill = sem("s_fill")
        s_src = sem("s_src")
        s_srcf = sem("s_srcf")
        s_const = sem("s_const")
        s_zero = sem("s_zero")
        s_table = [sem(f"s_table{j}") for j in range(TILES)]
        s_attr = [sem(f"s_attr{a}") for a in range(2)]
        s_tail0 = sem("s_tail0")
        s_tail = sem("s_tail")
        s_w = sem("s_w")
        s_w2 = sem("s_w2")
        s_bias_p = sem("s_bias_p")
        s_bias = sem("s_bias")
        s_x = sem("s_x")
        s_staged = sem("s_staged")
        s_rows = sem("s_rows")
        s_same = sem("s_same")
        s_sums = sem("s_sums")
        s_wsame = sem("s_wsame")
        s_weight = sem("s_weight")
        s_dup = sem("s_dup")
        s_idx = sem("s_idx")
        s_pay = sem("s_pay")
        s_sent = sem("s_sent")
        s_xstage = sem("s_xstage")
        s_xb = sem("s_xb")
        s_xt_p = sem("s_xt_p")
        s_xt = sem("s_xt")
        s_pre_p = sem("s_pre_p")
        s_pre = sem("s_pre")
        s_own = sem("s_own")
        s_own_dve = sem("s_own_dve")
        s_own_pe = sem("s_own_pe")
        s_part0 = [sem(f"s_part0_{j}") for j in range(TILES)]
        s_acc0 = sem("s_acc0")
        s_part = sem("s_part")
        s_acc = sem("s_acc")
        s_rc = sem("s_rc")
        s_agg = sem("s_agg")
        s_aggt_p = sem("s_aggt_p")
        s_aggt = sem("s_aggt")
        s_h_p = sem("s_h_p")
        s_hsum = sem("s_hsum")
        s_h = sem("s_h")
        s_y = sem("s_y")
        s_z = sem("s_z")
        s_stats = sem("s_stats")
        s_mv = sem("s_mv")
        s_std = sem("s_std")
        s_rstd = sem("s_rstd")
        s_shift = sem("s_shift")
        s_out = sem("s_out")
        s_store = sem("s_store")
        s_stored = sem("s_stored")

        block = ctx.enter_context(nc.Block())

        @block.sync
        def _(sp):
            sp.wait_ge(s_fill, 1)
            with nc.allow_non_contiguous_dma(reason="one edge per partition"):
                sp.dma_start(src_i[:, 0:MAIN_COLS], src_main).then_inc(s_src, 16)
                for t in range(LAST_TILES):
                    n = P if t < LAST_TILES - 1 else LAST_ROWS
                    at = MAIN_EDGES + t * P
                    sp.dma_start(src_i[0:n, MAIN_COLS + t:MAIN_COLS + t + 1],
                                 src[at:at + n].rearrange("(p o) -> p o", o=1)).then_inc(s_src, 16)

            def load_attr(i, a):
                first = (i * 2 + a) * (2 * TILES * FEAT)
                sp.dma_start(attr_s[a], attr_main[:, bass.ds(first, 2 * TILES * FEAT)]).then_inc(s_attr[a], 16)

            for a in range(2):
                load_attr(0, a)
            for j in range(TILES):
                sp.wait_ge(s_table[j], 16)
            sp.dma_start(w1x[:, :, :], w1[0:DIM, :].rearrange("(k p) n -> p k n", p=P)).then_inc(s_w, 16)
            sp.dma_start(w1u, w1[DIM + FEAT:DIM + FEAT + P, :]).then_inc(s_w, 16)
            with nc.allow_non_contiguous_dma(reason="a vector down the partitions"):
                sp.dma_start(u_col[:, :], u[0, :].rearrange("(p o) -> p o", o=1)).then_inc(s_w, 16)
                sp.dma_start(b1_col[:, :], b1.rearrange("(k p) -> p k", p=P)).then_inc(s_w, 16)
            sp.dma_start(b2_all[:, :], b2.partition_broadcast(P)).then_inc(s_w, 16)
            sp.dma_start(w1e[:, :], w1[DIM:DIM + FEAT, :]).then_inc(s_w2, 16)
            sp.dma_start(w2s[:, :, :], w2.rearrange("(k p) n -> p k n", p=P)).then_inc(s_w2, 16)

            def next_attr(i):
                for a in range(2):
                    sp.wait_ge(s_sums, i * UNITS - UNITS + 2 * a + 2 + SUM_SLOTS)
                    load_attr(i, a)

            with sp.Fori(1, X_PIECES + 1) as i:
                next_attr(i)
                for lo, hi in ((0, XPART), (XPART, NP)):
                    sp.dma_start(xs[lo:hi, bass.ds(i * X_PIECE - X_PIECE, X_PIECE)],
                                 x_v[lo:hi, bass.ds(i * X_PIECE - X_PIECE, X_PIECE)]).then_inc(s_x, 16)
            with sp.Fori(X_PIECES + 1, TURNS) as i:
                next_attr(i)
            sp.wait_ge(s_tail0, 1)
            for t in range(LAST_TILES):
                n = P if t < LAST_TILES - 1 else LAST_ROWS
                at = MAIN_EDGES + t * P
                sp.dma_start(attr_s[0][0:n, t * FEAT:(t + 1) * FEAT], attr[at:at + n, :]).then_inc(s_tail, 16)

            for j in FINAL_ORDER:
                uses = 1 + TURNS * UNITS + (1 if j < LAST_TILES else 0)
                sp.wait_ge(s_table[j], 16 * uses)
                sp.dma_start(partial[:, j * CHUNK_ROW:(j + 1) * CHUNK_ROW],
                             table_v[j][:, 0:CHUNK_ROW]).then_inc(s_part0[j], 16)

            def store_step(g, b):
                sp.wait_ge(s_out, g * 2 + 2)
                for lo, hi in ((0, XPART), (XPART, NP)):
                    sp.dma_start(out_v[lo:hi, bass.ds(g * (2 * DIM), 2 * DIM)],
                                 z[b][lo:hi, :]).then_inc(s_store, 16)
                sp.wait_ge(s_store, g * 32 + 32)
                sp.sem_inc(s_stored, 1)

            sp.sem_inc(s_stored, 2)
            with sp.Fori(0, PAIRS) as m:
                for s in range(PAIR):
                    store_step(m * PAIR + s, s % 2)
            for g in range(PAIRS * PAIR, STEPS):
                store_step(g, g % 2)

        @block.gpsimd
        def _(pool):
            nc.gpsimd.iota(src_i[:, MAIN_COLS:SRC_COLS], pattern=[[0, LAST_TILES]], base=NODES,
                           channel_multiplier=1)
            nc.gpsimd.iota(spare_i[:, :], pattern=[[0, 1]], base=NODES, channel_multiplier=1).then_inc(s_fill, 1)
            pool.sem_inc(s_sent, OUT_SLOTS - 1)
            nc.gpsimd.memset(eps_col[:, :], EPS).then_inc(s_const, 1)
            nc.gpsimd.memset(ident[:, :], 0.0).then_inc(s_const, 1)
            nc.gpsimd.memset(same_weight[:, :], 1.0).then_inc(s_const, 1)
            pool.wait_ge(s_const, 3)
            nc.gpsimd.affine_select(out=ident[:, :], in_=ident[:, :], compare_op=ALU.not_equal, fill=1.0,
                                    base=0, pattern=[[-1, P]], channel_multiplier=1).then_inc(s_const, 1)
            nc.gpsimd.affine_select(out=same_weight[:, :], in_=same_weight[:, :], compare_op=ALU.is_ge, fill=DUP,
                                    base=0, pattern=[[1, P]], channel_multiplier=-1).then_inc(s_const, 1)
            pool.wait_ge(s_zero, 1)
            for j in range(TILES):
                pool.dma_start(table_v[j].rearrange("p (k w) -> p k w", k=CHUNKS),
                               partial[:, 0:CHUNK_ROW].unsqueeze(1).to_broadcast([P, CHUNKS, CHUNK_ROW])
                               ).then_inc(s_table[j], 16)

            def scatter_unit(n, s, tiles):
                pool.wait_ge(s_idx, n + (1 + OUT_SLOTS))
                pool.wait_ge(s_pay, n + (1 + SUM_SLOTS))
                for j in range(tiles):
                    pool.wait_ge(s_table[j], n * 16 + 16)
                    pool.sem_inc(s_own, 1)
                    d = pool.indirect_dma_start(
                        out=tables[j], out_offset=bass.IndirectOffsetOnAxis(ap=idx[s][:, j:j + 1], axis=0),
                        in_=payload[s][:, j, :], in_offset=None, compute_op=ALU.add,
                        engine_sem=s_sent if j == tiles - 1 else None)
                    d.then_inc(s_table[j], 16)

            with pool.Fori(0, TURNS) as i:
                for s in range(UNITS):
                    scatter_unit(i * UNITS + s, s, TILES)
            scatter_unit(TURNS * UNITS, 0, LAST_TILES)

            def add_tables(k, b):
                pool.wait_ge(s_aggt_p, k * CHUNK_STEPS + CHUNK_STEPS)
                for j in range(1, TILES):
                    if j > 1:
                        pool.wait_ge(s_acc, (k - 1) * (TILES - 1) + (j - 1))
                    nc.gpsimd.tensor_tensor(acc[b], partial[:, 0:CHUNK_ROW] if j == 1 else acc[b],
                                            partial[:, j * CHUNK_ROW:(j + 1) * CHUNK_ROW],
                                            ALU.add).then_inc(s_acc, 1)

            def load_chunk(k):
                if k > 1:
                    pool.wait_ge(s_acc, (k - 1) * (TILES - 1))
                for j in range(TILES):
                    pool.dma_start(partial[:, j * CHUNK_ROW:(j + 1) * CHUNK_ROW],
                                   table_v[j][:, bass.ds(k * CHUNK_ROW, CHUNK_ROW)]).then_inc(s_part, 16)

            pool.wait_ge(s_acc0, TILES - 1)
            for k in range(1, CHUNKS):
                load_chunk(k)
                pool.wait_ge(s_part, k * (16 * TILES))
                add_tables(k, k % 2)

        @block.scalar
        def _(act):
            act.sem_inc(s_pay, SUM_SLOTS)
            act.sem_inc(s_xt, 1)
            act.wait_ge(s_srcf, 2)

            def stage(n, s, tiles=TILES):
                act.wait_ge(s_idx, n + 1)
                first = n * TILES
                nc.scalar.copy(src_unit[s][:, 0:tiles], srcf[:, bass.ds(first, tiles)]).then_inc(s_staged, 1)

            def evacuate(n, s, tiles=TILES):
                act.wait_ge(s_sums, n + (1 + SUM_SLOTS))
                act.wait_ge(s_idx, n + (1 + OUT_SLOTS))
                nc.scalar.copy(payload[s][:, 0:tiles, 0:FEAT],
                               sums_p[s % 2][:, 0:tiles * FEAT].rearrange("p (t f) -> p t f", f=FEAT)
                               ).then_inc(s_pay, 1)

            def stage_x(d, q):
                act.wait_ge(s_xb, d + 1)
                act.wait_ge(s_xt_p, d + 1)
                nc.scalar.copy(x_stage[q][0:NP, :], xs[0:NP, bass.ds(d * DIM, DIM)]).then_inc(s_xstage, 1)

            def save_xt(d):
                act.wait_ge(s_xt_p, d + 3)
                act.wait_ge(s_pre_p, d + 1)
                nc.scalar.copy(xt[:, :, :], xt_p.rearrange("p (k n) -> p k n", n=NP)).then_inc(s_xt, 1)

            def turn(i, dense_at):
                n = i * UNITS
                if dense_at is not None:
                    stage_x(dense_at, 0)
                stage(n, 0)
                stage(n + 1, 1)
                if dense_at is not None:
                    save_xt(dense_at)
                    stage_x(dense_at + 1, 1)
                evacuate(n, 0)
                stage(n + 2, 2)
                evacuate(n + 1, 1)
                if dense_at is not None:
                    save_xt(dense_at + 1)
                stage(n + 3, 3)
                evacuate(n + 2, 2)
                evacuate(n + 3, 3)

            with act.Fori(0, PLAIN_TURNS) as i:
                turn(i, None)
            act.wait_ge(s_x, 2 * 16 * X_PIECES)
            with act.Fori(PLAIN_TURNS, TURNS) as i:
                turn(i, i * 2 - 2 * PLAIN_TURNS)
            stage(TURNS * UNITS, 0, LAST_TILES)
            evacuate(TURNS * UNITS, 0, LAST_TILES)

            act.sem_inc(s_aggt, 2)

            def save_aggt(g, b):
                act.wait_ge(s_aggt_p, g + (1 + PAIR))
                act.wait_ge(s_h_p, g + 1)
                nc.scalar.copy(aggt[b][0:FEAT, :], aggt_p[b]).then_inc(s_aggt, 1)

            def relu(g, b):
                act.wait_ge(s_hsum, g * 2 + (2 + 4))
                nc.scalar.activation(h_s[b], h_s[b], ACT.Relu).then_inc(s_h, 1)

            def normalize(g, b):
                act.wait_ge(s_mv, g * 2 + 2)
                nc.scalar.activation(std[0:NP, b, :], mv[0:NP, b, :, 1], ACT.Sqrt,
                                     bias=eps_col[0:NP, :]).then_inc(s_std, 1)
                act.wait_ge(s_shift, g + 1)
                for c in range(2):
                    nc.scalar.activation(z[b][0:NP, c * DIM:(c + 1) * DIM], z[b][0:NP, c * DIM:(c + 1) * DIM],
                                         ACT.Identity, scale=rstd[0:NP, b, c:c + 1],
                                         bias=shift[0:NP, b, c:c + 1]).then_inc(s_out, 1)

            def step(g, b, left=STEPS):
                if left > 2:
                    save_aggt(g + 2, b)
                if left > 1:
                    relu(g + 1, 1 - b)
                normalize(g, b)

            save_aggt(0, 0)
            save_aggt(1, 1)
            relu(0, 0)
            with act.Fori(0, PAIRS) as m:
                for s in range(PAIR):
                    step(m * PAIR + s, s % 2)
            for g in range(PAIRS * PAIR, STEPS):
                step(g, g % 2, STEPS - g)

        @block.tensor
        def _(pe):
            pe.sem_inc(s_sums, SUM_SLOTS)
            pe.sem_inc(s_aggt_p, PAIR)
            pe.sem_inc(s_xt_p, 2)
            pe.sem_inc(s_pre_p, 1)
            pe.wait_ge(s_const, 5)

            def spread(n, s, tiles=TILES):
                pe.wait_ge(s_staged, n + 1)
                pe.wait_ge(s_same, n + 1)
                for t in range(tiles):
                    last = nc.tensor.transpose(rows_p[s % 2][:, t * P:(t + 1) * P],
                                               src_unit[s][:, t:t + 1].to_broadcast([P, P]), ident[:, :])
                last.then_inc(s_rows, 1)

            def add_up(n, s, tiles=TILES):
                pe.wait_ge(s_same, n + (1 + ROWS_SLOTS))
                pe.wait_ge(s_pay, n + 1)
                for t in range(tiles):
                    at = (s % 2 * TILES + t) * FEAT
                    last = nc.tensor.matmul(sums_p[s % 2][:, t * FEAT:(t + 1) * FEAT], same[s % 2][:, t, :],
                                            attr_s[s // 2][:, at:at + FEAT], start=True, stop=True)
                last.then_inc(s_sums, 1)

            def transpose_x(d, q):
                pe.wait_ge(s_xstage, d + 1)
                pe.wait_ge(s_xt, d + 1)
                for k in range(KX):
                    last = nc.tensor.transpose(xt_p[:, k * NP:(k + 1) * NP], x_stage[q][0:NP, k * P:(k + 1) * P],
                                               ident[0:NP, 0:NP])
                last.then_inc(s_xt_p, 1)

            def first_layer_x(d):
                pe.wait_ge(s_xt, d + 2)
                pe.wait_ge(s_pre, d + 1)
                for k in range(KH):
                    for c in range(KX):
                        last = nc.tensor.matmul(pre_p[:, k * NP:(k + 1) * NP], w1x[:, c, k * P:(k + 1) * P],
                                                xt[:, c, :], start=(c == 0), stop=(c == KX - 1))
                last.then_inc(s_pre_p, 1)

            def turn(i, d):
                n = i * UNITS
                spread(n, 0)
                if d is not None:
                    transpose_x(d, 0)
                pe.wait_ge(s_attr[0], i * 16 + 16)
                add_up(n, 0)
                spread(n + 1, 1)
                if d is not None:
                    first_layer_x(d)
                    transpose_x(d + 1, 1)
                add_up(n + 1, 1)
                spread(n + 2, 2)
                pe.wait_ge(s_attr[1], i * 16 + 16)
                add_up(n + 2, 2)
                if d is not None:
                    first_layer_x(d + 1)
                spread(n + 3, 3)
                add_up(n + 3, 3)

            with pe.Fori(0, PLAIN_TURNS) as i:
                turn(i, None)
            pe.wait_ge(s_w, 5 * 16)
            for k in range(KH):
                last = nc.tensor.matmul(bias_p[:, k:k + 1], w1u[:, k * P:(k + 1) * P], u_col[:, :],
                                        start=True, stop=True)
            last.then_inc(s_bias_p, 1)
            with pe.Fori(PLAIN_TURNS, TURNS) as i:
                turn(i, i * 2 - 2 * PLAIN_TURNS)
            spread(TURNS * UNITS, 0, LAST_TILES)
            pe.wait_ge(s_tail, 16 * LAST_TILES)
            add_up(TURNS * UNITS, 0, LAST_TILES)

            pe.wait_ge(s_pay, ALL_UNITS + SUM_SLOTS)
            pe.wait_ge(s_pre, COLS + 1)
            pe.wait_ge(s_w2, 2 * 16)
            pe.sem_inc(s_h_p, 2)
            pe.sem_inc(s_y, 2)

            def transpose_means(g, b, s):
                pe.wait_ge(s_aggt, g + 1)
                pe.sem_inc(s_own_pe, 1)
                means = acc[s // CHUNK_STEPS % 2].rearrange("p (c r) -> p c r", r=ROW)
                for c in range(2):
                    last = nc.tensor.transpose(aggt_p[b][:, c * NP:(c + 1) * NP],
                                               means[0:NP, s % CHUNK_STEPS * 2 + c, 0:FEAT], ident[0:NP, 0:NP])
                last.then_inc(s_aggt_p, 1)

            def first_layer_edges(g, b):
                pe.wait_ge(s_aggt, g + 3)
                pe.wait_ge(s_hsum, g * 2 + 2)
                for k in range(KH):
                    at = k // 2 * 512 + k % 2 * NW
                    last = nc.tensor.matmul(h_p[b][:, at:at + NW], w1e[:, k * P:(k + 1) * P],
                                            aggt[b][0:FEAT, :], start=True, stop=True)
                last.then_inc(s_h_p, 1)

            def second_layer(g, b):
                pe.wait_ge(s_h, g + 1)
                pe.wait_ge(s_z, g * 2 + 2)
                for c in range(2):
                    for k in range(KH):
                        at = k * NW + c * NP
                        last = nc.tensor.matmul(y_p[b][0:NP, c * DIM:(c + 1) * DIM], h_s[b][:, at:at + NP],
                                                w2s[:, k, :], start=(k == 0), stop=(k == KH - 1))
                last.then_inc(s_y, 1)

            def step(m, s, left=STEPS):
                g = m * PAIR + s
                b = s % 2
                if left > 2:
                    ahead = s + 2
                    if ahead % CHUNK_STEPS == 0:
                        pe.wait_ge(s_agg, m * 2 + (ahead // CHUNK_STEPS + 1))
                    transpose_means(g + 2, b, ahead)
                if left > 1:
                    first_layer_edges(g + 1, 1 - b)
                second_layer(g, b)

            pe.wait_ge(s_agg, 1)
            transpose_means(0, 0, 0)
            transpose_means(1, 1, 1)
            first_layer_edges(0, 0)
            with pe.Fori(0, PAIRS) as m:
                for s in range(PAIR):
                    step(m, s)
            for g in range(PAIRS * PAIR, STEPS):
                step(PAIRS, g - PAIRS * PAIR, STEPS - g)

        @block.vector
        def _(dve):
            dve.sem_inc(s_same, ROWS_SLOTS)
            dve.sem_inc(s_idx, OUT_SLOTS)
            dve.sem_inc(s_xb, 2)
            dve.sem_inc(s_pre, 1)
            nc.vector.memset(partial[:, 0:CHUNK_ROW], 0.0).then_inc(s_zero, 1)
            dve.wait_ge(s_src, 16 * (1 + LAST_TILES))
            nc.vector.tensor_copy(srcf[:, :], src_i).then_inc(s_srcf, 1)
            nc.vector.tensor_copy(spare_row[:, :], spare_i[:, :]).then_inc(s_srcf, 1)
            dve.wait_ge(s_srcf, 2)
            dve.wait_ge(s_const, 5)

            def mark(n, s, tiles=TILES):
                b = s % 2
                ids = src_unit[s][:, 0:tiles]
                dve.wait_ge(s_rows, n + 1)
                dve.wait_ge(s_sums, n + 1)
                nc.vector.tensor_tensor(same[b][:, 0:tiles, :],
                                        rows_p[b][:, 0:tiles * P].rearrange("p (t e) -> p t e", e=P),
                                        ids.unsqueeze(2).to_broadcast([P, tiles, P]),
                                        ALU.is_equal).then_inc(s_same, 1)
                dve.wait_ge(s_same, n + (1 + ROWS_SLOTS))
                nc.vector.tensor_tensor(wsame[:, 0:tiles, :], same[b][:, 0:tiles, :],
                                        same_weight[:, :].unsqueeze(1).to_broadcast([P, tiles, P]),
                                        ALU.mult).then_inc(s_wsame, 1)
                dve.wait_ge(s_wsame, n + 1)
                dve.wait_ge(s_sent, n + 1)
                count = payload[s][:, 0:tiles, FEAT:ROW]
                nc.vector.tensor_reduce(count, wsame[:, 0:tiles, :], AX.X, ALU.add).then_inc(s_weight, 1)
                dve.wait_ge(s_weight, n + 1)
                nc.vector.tensor_scalar(t_dup[:, 0:tiles].unsqueeze(2), count, DUP, spare_row[:, 0:1],
                                        ALU.is_ge, ALU.mult).then_inc(s_dup, 1)
                dve.wait_ge(s_dup, n + 1)
                nc.vector.tensor_tensor(idx[s][:, 0:tiles], t_dup[:, 0:tiles], ids, ALU.max).then_inc(s_idx, 1)

            def add_b2(d, q):
                dve.wait_ge(s_xstage, d + 1)
                nc.vector.tensor_tensor(xs[0:NP, bass.ds(d * DIM, DIM)], x_stage[q][0:NP, :], b2_all[0:NP, :],
                                        ALU.add).then_inc(s_xb, 1)

            def save_pre(d):
                dve.wait_ge(s_pre_p, d + 2)
                nc.vector.tensor_tensor(pre[:, bass.ds(d * (KH * NP), KH * NP)].rearrange("p (k n) -> p k n", n=NP),
                                        pre_p.rearrange("p (k n) -> p k n", n=NP),
                                        hid_bias[:, :].unsqueeze(2).to_broadcast([P, KH, NP]),
                                        ALU.add).then_inc(s_pre, 1)

            def turn(i, d):
                n = i * UNITS
                mark(n, 0)
                if d is not None:
                    add_b2(d, 0)
                mark(n + 1, 1)
                if d is not None:
                    add_b2(d + 1, 1)
                    save_pre(d)
                mark(n + 2, 2)
                if d is not None:
                    save_pre(d + 1)
                mark(n + 3, 3)

            with dve.Fori(0, PLAIN_TURNS) as i:
                turn(i, None)
            dve.wait_ge(s_w, 5 * 16)
            dve.wait_ge(s_bias_p, 1)
            nc.vector.tensor_tensor(hid_bias[:, :], bias_p, b1_col[:, :], ALU.add).then_inc(s_bias, 1)
            dve.wait_ge(s_bias, 1)
            with dve.Fori(PLAIN_TURNS, TURNS) as i:
                turn(i, i * 2 - 2 * PLAIN_TURNS)
            dve.wait_ge(s_sums, TURNS * UNITS + SUM_SLOTS - 2)
            nc.vector.memset(attr_s[0][:, (LAST_TILES - 1) * FEAT:LAST_TILES * FEAT], 0.0).then_inc(s_tail0, 1)
            mark(TURNS * UNITS, 0, LAST_TILES)

            dve.sem_inc(s_hsum, 4)
            dve.sem_inc(s_z, 4)

            def part(j):
                return partial[:, j * CHUNK_ROW:(j + 1) * CHUNK_ROW]

            def chunk_means(k, b):
                rows = acc[b].rearrange("p (c r) -> p c r", r=ROW)
                nc.vector.tensor_scalar(rcount[:, :].unsqueeze(2), rows[:, :, FEAT:ROW], 1.0, None,
                                        ALU.max).then_inc(s_rc, 1)
                dve.wait_ge(s_rc, k * 2 + 1)
                nc.vector.reciprocal(rcount[:, :], rcount[:, :]).then_inc(s_rc, 1)
                dve.wait_ge(s_rc, k * 2 + 2)
                nc.vector.tensor_tensor(rows[:, :, 0:FEAT], rows[:, :, 0:FEAT],
                                        rcount[:, :].unsqueeze(2).to_broadcast([P, CC, FEAT]),
                                        ALU.mult).then_inc(s_agg, 1)

            def hidden_sum(g, b):
                dve.wait_ge(s_h_p, g + 3)
                dve.wait_ge(s_y, g + 1)
                both = pre[:, bass.ds(g * (2 * KH * NP), 2 * KH * NP)].rearrange("p (c k n) -> p k c n", c=2, n=NP)
                for r in range(2):
                    nc.vector.tensor_tensor(
                        h_s[b][:, r * 2 * NW:(r + 1) * 2 * NW].rearrange("p (k c n) -> p k c n", k=2, c=2),
                        h_p[b][:, r * 512:r * 512 + 2 * NW].rearrange("p (k c n) -> p k c n", k=2, c=2),
                        both[:, 2 * r:2 * r + 2, :, :], ALU.add).then_inc(s_hsum, 1)

            def layer_norm(g, b):
                dve.wait_ge(s_y, g + 3)
                dve.wait_ge(s_stored, g + 1)
                for c in range(2):
                    nc.vector.tensor_tensor(z[b][0:NP, c * DIM:(c + 1) * DIM], y_p[b][0:NP, c * DIM:(c + 1) * DIM],
                                            xs[0:NP, bass.ds(g * (2 * DIM) + c * DIM, DIM)],
                                            ALU.add).then_inc(s_z, 1)
                dve.wait_ge(s_z, g * 2 + (2 + 4))
                for c in range(2):
                    nc.vector.bn_stats(stats[0:NP, b, c, :], z[b][0:NP, c * DIM:(c + 1) * DIM]).then_inc(s_stats, 1)
                dve.wait_ge(s_stats, g * 2 + 2)
                dve.sem_inc(s_own_dve, 1)
                for c in range(2):
                    nc.vector.bn_aggr(mv[0:NP, b, c, :], stats[0:NP, b, c, :]).then_inc(s_mv, 1)
                dve.wait_ge(s_std, g + 1)
                nc.vector.reciprocal(rstd[0:NP, b, :], std[0:NP, b, :]).then_inc(s_rstd, 1)
                dve.wait_ge(s_rstd, g + 1)
                nc.vector.scalar_tensor_tensor(shift[0:NP, b, :], mv[0:NP, b, :, 0], -1.0, rstd[0:NP, b, :],
                                               ALU.mult, ALU.mult).then_inc(s_shift, 1)

            def step(m, s, left=STEPS):
                g = m * PAIR + s
                if left > 1:
                    hidden_sum(g + 1, (s + 1) % 2)
                if s % CHUNK_STEPS == 1 and left > CHUNK_STEPS:
                    k = s // CHUNK_STEPS + 1
                    dve.wait_ge(s_acc, (m * 2 + k) * (TILES - 1))
                    chunk_means(m * 2 + k, k % 2)
                layer_norm(g, s % 2)

            a, b, *others = FINAL_ORDER
            dve.wait_ge(s_part0[a], 16)
            dve.wait_ge(s_part0[b], 16)
            nc.vector.tensor_tensor(acc[0], part(a), part(b), ALU.add).then_inc(s_acc0, 1)
            for n, j in enumerate(others):
                dve.wait_ge(s_part0[j], 16)
                dve.wait_ge(s_acc0, n + 1)
                nc.vector.tensor_tensor(acc[0], acc[0], part(j), ALU.add).then_inc(s_acc0, 1)
            dve.wait_ge(s_acc0, TILES - 1)
            chunk_means(0, 0)
            hidden_sum(0, 0)
            with dve.Fori(0, PAIRS) as m:
                for s in range(PAIR):
                    step(m, s)
            for g in range(PAIRS * PAIR, STEPS):
                step(PAIRS, g - PAIRS * PAIR, STEPS - g)


_INS = ["x", "src", "edge_attr_64", "L0_gnn_u", "L0_gnn_W1", "L0_gnn_b1", "L0_gnn_W2", "L0_gnn_b2"]


def kernel(**inputs):
    import numpy as _np
    import concourse.bacc as _bacc
    from concourse import mybir as _mybir
    from concourse.bass_utils import run_bass_kernel_spmd as _run

    nc = _bacc.Bacc("TRN2", target_bir_lowering=False, num_devices=1)
    arrays, args = {}, []
    for name in _INS:
        a = _np.ascontiguousarray(inputs[name])
        arrays[f"in_{name}"] = a
        args.append(nc.dram_tensor(f"in_{name}", a.shape, _mybir.dt.from_np(a.dtype), kind="ExternalInput").ap())
    out = nc.dram_tensor("out_0", (NODES, DIM), F32, kind="ExternalOutput").ap()
    build(nc, *args, out)
    r = _run(nc, [arrays], core_ids=[0])
    return r.results[0]["out_0"]
```

```python
from contextlib import ExitStack

import concourse.bass as bass
from concourse import mybir

F32 = mybir.dt.float32
BF16 = mybir.dt.bfloat16
I16 = mybir.dt.int16
I32 = mybir.dt.int32
U32 = mybir.dt.uint32
ALU = mybir.AluOpType
ACT = mybir.ActivationFunctionType
AX = mybir.AxisListType

P = 128
NODES, DIM = 6250, 256
EDGES, FEAT = 100000, 64
HID = 512
EPS = 1e-5

ROW = FEAT + 1
TILES = 5
UNITS = 4
UNIT_EDGES = P * TILES
FULL_COLS = EDGES // P
PART_ROWS = EDGES - FULL_COLS * P
TURNS = 35
PASS_TURNS = 17
DIRECT = 4
DIRECT_COLS = PASS_TURNS * DIRECT
POOL_COLS = FULL_COLS - DIRECT_COLS
END_COLS = POOL_COLS - TURNS * UNITS * TILES
END_UNITS = [TILES, TILES, END_COLS + 1 - 2 * TILES]
N_END = TURNS * UNITS
assert 0 < END_UNITS[2] <= TILES and PART_ROWS > 0
ALL_UNITS = N_END + len(END_UNITS)
SRC_COLS = FULL_COLS + 1
FINAL_ORDER = [*range(END_UNITS[2], TILES), *range(END_UNITS[2])]
SUM_TABLE = TILES - 1
HALVES = [(0, 13), (13, 12), (25, 13), (38, 12)]
OH_COLS = 13
BANK_COLS = 512 // ROW
DUP = 256.0

NP = 125
COLS = NODES // NP
TABLE_ROWS = P * COLS
XPART = 112
KX = DIM // P
KH = HID // P
PASS_COLS = COLS // 2
DENSE_TURNS = COLS // 2
PLAIN_TURNS = TURNS - DENSE_TURNS
X_PIECES = 10
X_PIECE = COLS * DIM // X_PIECES
assert X_PIECES <= PLAIN_TURNS
CHUNKS = 5
CC = COLS // CHUNKS
CHUNK_STEPS = CC // 2
STEPS = COLS // 2
PAIR = 2 * CHUNK_STEPS
PAIRS = STEPS // PAIR
CHUNK_ROW = CC * ROW
NW = 2 * NP

SAME_SLOTS = 2
SUM_SLOTS = 1
OUT_SLOTS = 4


def build(nc, x, src, attr, u, w1, b1, w2, b2, out):
    tables = [nc.dram_tensor(f"table{j}", [TABLE_ROWS, ROW], F32, kind="Internal").ap()
              for j in range(TILES)]
    src_main = src[0:FULL_COLS * P].rearrange("(p t) -> p t", p=P)
    attr_main = attr[0:FULL_COLS * P, :].rearrange("(p t) f -> p (t f)", p=P)
    x_v = x.rearrange("(p c) d -> p (c d)", p=NP)
    out_v = out.rearrange("(p c) d -> p (c d)", p=NP)
    table_v = [t.rearrange("(p c) r -> p (c r)", p=P) for t in tables]

    ctx = ExitStack()
    with ctx:
        def sb(name, shape, dt=F32):
            return ctx.enter_context(nc.sbuf_tensor(name, shape, dt))

        def pb(name, shape, dt=F32):
            return ctx.enter_context(nc.psum_tensor(name, shape, dt))

        def sem(name):
            return ctx.enter_context(nc.semaphore(name))

        ident = sb("ident", [P, P])
        same_weight = sb("same_weight", [P, P])
        spare_row = sb("spare_row", [P, 1])
        spare_i = sb("spare_i", [P, 1], I32)
        w1x = sb("w1x", [P, KX, HID])
        w1e = sb("w1e", [FEAT, HID])
        w2s = sb("w2s", [P, KH, DIM])
        b2_all = sb("b2_all", [P, DIM])
        b1_col = sb("b1_col", [P, KH])
        u_col = sb("u_col", [P, 1])
        hid_bias = sb("hid_bias", [P, KH])

        xs = sb("xs", [P, COLS * DIM])
        pre = sb("pre", [P, COLS * HID // P * NP])
        x_stage = [sb(f"x_stage{q}", [P, DIM]) for q in range(2)]
        xt = sb("xt", [P, KX, NP])
        partial = sb("partial", [P, TILES * CHUNK_ROW])
        rcount = sb("rcount", [P, CC])
        stats = sb("stats", [P, 2, 2, 6])
        mv = sb("mv", [P, 2, 2, 2])
        std = sb("std", [P, 2, 2])
        rstd = sb("rstd", [P, 2, 2])
        shift = sb("shift", [P, 2, 2])
        eps_col = sb("eps_col", [P, 1])

        srcf = sb("srcf", [P, SRC_COLS])
        src_unit = [sb(f"src_unit{s}", [P, TILES]) for s in range(UNITS)]
        t_dup = sb("t_dup", [P, TILES])
        idx = [sb(f"idx{s}", [P, TILES], U32) for s in range(UNITS)]
        A_ATTR, A_SAME = 0, 2 * TILES * FEAT * 2
        A_WSAME = A_SAME + 2 * TILES * P
        A_PAY = A_WSAME + TILES * P
        A_END = A_PAY + UNITS * TILES * ROW
        area = sb("area", [P, A_END])
        attr_s = [area[:, A_ATTR + a * 2 * TILES * FEAT:A_ATTR + (a + 1) * 2 * TILES * FEAT] for a in range(2)]
        same = [area[:, A_SAME + b * TILES * P:A_SAME + (b + 1) * TILES * P].rearrange("p (t e) -> p t e", e=P)
                for b in range(2)]
        wsame = area[:, A_WSAME:A_PAY].rearrange("p (t e) -> p t e", e=P)
        payload = [area[:, A_PAY + s * TILES * ROW:A_PAY + (s + 1) * TILES * ROW].rearrange("p (t r) -> p t r", r=ROW)
                   for s in range(UNITS)]
        at = 0
        node_area = []
        for length in (KH * NW, 2 * DIM, NW, CHUNK_ROW // 2):
            node_area.append([area[:, at + b * length:at + (b + 1) * length] for b in range(2)])
            at += 2 * length
        h_s, z, aggt, _ = node_area
        acc = [sb("acc0", [P, CHUNK_ROW])[:, :], area[:, at - CHUNK_ROW:at]]
        assert at <= A_END
        src_i = pre[:, 0:SRC_COLS].bitcast(I32)
        w1u = pre[:, 1024:1024 + HID]

        raw = [acc[0][:, g * 2 * FEAT:(g + 1) * 2 * FEAT].rearrange("p (t f) -> p t f", f=FEAT) for g in range(2)]
        PART_LEN = 3 * FEAT + 2
        parts = [sb(f"parts{g}", [P, 2, PART_LEN], BF16) for g in range(2)]
        node_of = sb("node_of", [P, OH_COLS * P], I16)
        src_direct = sb("src_direct", [P, len(HALVES), DIRECT_COLS])
        zeros = sb("zeros", [P, P], BF16)
        direct_sum = partial[:, 0:PASS_COLS * ROW]
        onehot = [partial[:, at:at + cols * P // 2].bitcast(BF16)
                  for at, cols in ((PASS_COLS * ROW, HALVES[0][1]),
                                   (PASS_COLS * ROW + HALVES[0][1] * P // 2, HALVES[1][1]))]
        assert PASS_COLS * (ROW + P // 2) <= TILES * CHUNK_ROW

        ps = pb("ps", [P, 8 * 512])
        rows_p = ps[:, 0:TILES * P]
        sums_p = ps[:, 2 * 512:2 * 512 + TILES * FEAT]
        bias_p = ps[:, 3 * 512:3 * 512 + KH]
        xt_p = ps[:, 3 * 512:3 * 512 + KX * NP]
        pre_p = ps[:, 3 * 512:3 * 512 + KH * NP]
        direct_p = [ps[:, (4 + g) * 512:(4 + g) * 512 + min(BANK_COLS, PASS_COLS - g * BANK_COLS) * ROW]
                    for g in range(-(-PASS_COLS // BANK_COLS))]
        h_p = [ps[:, 2 * b * 512:(2 * b + 2) * 512] for b in range(2)]
        y_p = [ps[:, (4 + b) * 512:(5 + b) * 512] for b in range(2)]
        aggt_p = [ps[0:FEAT, (6 + b) * 512:(6 + b) * 512 + NW] for b in range(2)]

        s_fill = sem("s_fill")
        s_src = sem("s_src")
        s_srcf = sem("s_srcf")
        s_const = sem("s_const")
        s_zero = sem("s_zero")
        s_table = [sem(f"s_table{j}") for j in range(TILES)]
        s_attr = [sem(f"s_attr{a}") for a in range(2)]
        s_tail0 = sem("s_tail0")
        s_tail = sem("s_tail")
        s_raw = [sem(f"s_raw{g}") for g in range(2)]
        s_hi = sem("s_hi")
        s_rest = sem("s_rest")
        s_mid = sem("s_mid")
        s_lo = sem("s_lo")
        s_direct = sem("s_direct")
        s_onehot = sem("s_onehot")
        s_used = sem("s_used")
        s_pass = sem("s_pass")
        s_pass_out = sem("s_pass_out")
        s_w = sem("s_w")
        s_w2 = sem("s_w2")
        s_bias_p = sem("s_bias_p")
        s_bias = sem("s_bias")
        s_x = sem("s_x")
        s_staged = sem("s_staged")
        s_rows = sem("s_rows")
        s_same = sem("s_same")
        s_sums = sem("s_sums")
        s_wsame = sem("s_wsame")
        s_weight = sem("s_weight")
        s_dup = sem("s_dup")
        s_idx = sem("s_idx")
        s_pay = sem("s_pay")
        s_sent = sem("s_sent")
        s_xstage = sem("s_xstage")
        s_xb = sem("s_xb")
        s_xt_p = sem("s_xt_p")
        s_xt = sem("s_xt")
        s_pre_p = sem("s_pre_p")
        s_pre = sem("s_pre")
        s_own = sem("s_own")
        s_own_dve = sem("s_own_dve")
        s_own_pe = sem("s_own_pe")
        s_part0 = [sem(f"s_part0_{j}") for j in range(TILES)]
        s_acc0 = sem("s_acc0")
        s_part = sem("s_part")
        s_acc = sem("s_acc")
        s_rc = sem("s_rc")
        s_agg = sem("s_agg")
        s_aggt_p = sem("s_aggt_p")
        s_aggt = sem("s_aggt")
        s_h_p = sem("s_h_p")
        s_hsum = sem("s_hsum")
        s_h = sem("s_h")
        s_y = sem("s_y")
        s_z = sem("s_z")
        s_stats = sem("s_stats")
        s_mv = sem("s_mv")
        s_std = sem("s_std")
        s_rstd = sem("s_rstd")
        s_shift = sem("s_shift")
        s_out = sem("s_out")
        s_store = sem("s_store")
        s_stored = sem("s_stored")

        block = ctx.enter_context(nc.Block())

        @block.sync
        def _(sp):
            sp.wait_ge(s_fill, 1)
            with nc.allow_non_contiguous_dma(reason="one edge per partition"):
                sp.dma_start(src_i[:, 0:POOL_COLS], src_main[:, 0:POOL_COLS]).then_inc(s_src, 16)
                sp.dma_start(src_i[:, POOL_COLS + 1:SRC_COLS], src_main[:, POOL_COLS:FULL_COLS]).then_inc(s_src, 16)
                sp.dma_start(src_i[0:PART_ROWS, POOL_COLS:POOL_COLS + 1],
                             src[FULL_COLS * P:EDGES].rearrange("(p o) -> p o", o=1)).then_inc(s_src, 16)

            def load_attr(i, a):
                first = (i * 2 + a) * (2 * TILES * FEAT)
                sp.dma_start(attr_s[a], attr_main[:, bass.ds(first, 2 * TILES * FEAT)]).then_inc(s_attr[a], 16)

            def load_raw(i, first):
                for g in range(2):
                    sp.wait_ge(s_lo, i * 2 + (g + 1))
                    at = POOL_COLS * FEAT + first * FEAT + g * 2 * FEAT
                    sp.dma_start(raw[g].rearrange("p t f -> p (t f)"),
                                 attr_main[:, bass.ds(at, 2 * FEAT)]).then_inc(s_raw[g], 16)

            for a in range(2):
                load_attr(0, a)
            load_raw(0, 0)
            for j in range(TILES):
                sp.wait_ge(s_table[j], 16)
            sp.dma_start(w1x[:, :, :], w1[0:DIM, :].rearrange("(k p) n -> p k n", p=P)).then_inc(s_w, 16)
            sp.dma_start(w1u, w1[DIM + FEAT:DIM + FEAT + P, :]).then_inc(s_w, 16)
            with nc.allow_non_contiguous_dma(reason="a vector down the partitions"):
                sp.dma_start(u_col[:, :], u[0, :].rearrange("(p o) -> p o", o=1)).then_inc(s_w, 16)
                sp.dma_start(b1_col[:, :], b1.rearrange("(k p) -> p k", p=P)).then_inc(s_w, 16)
            sp.dma_start(b2_all[:, :], b2.partition_broadcast(P)).then_inc(s_w, 16)
            sp.dma_start(w1e[:, :], w1[DIM:DIM + FEAT, :]).then_inc(s_w2, 16)
            sp.dma_start(w2s[:, :, :], w2.rearrange("(k p) n -> p k n", p=P)).then_inc(s_w2, 16)

            def next_attr(i):
                for a in range(2):
                    sp.wait_ge(s_sums, i * UNITS - UNITS + 2 * a + 2 + SAME_SLOTS)
                    load_attr(i, a)

            with sp.Fori(1, X_PIECES + 1) as i:
                next_attr(i)
                load_raw(i, i * DIRECT)
                for lo, hi in ((0, XPART), (XPART, NP)):
                    sp.dma_start(xs[lo:hi, bass.ds(i * X_PIECE - X_PIECE, X_PIECE)],
                                 x_v[lo:hi, bass.ds(i * X_PIECE - X_PIECE, X_PIECE)]).then_inc(s_x, 16)
            with sp.Fori(X_PIECES + 1, PASS_TURNS) as i:
                next_attr(i)
                load_raw(i, i * DIRECT)
            with sp.Fori(PASS_TURNS, 2 * PASS_TURNS) as i:
                next_attr(i)
                load_raw(i, i * DIRECT - DIRECT_COLS)
            for i in range(2 * PASS_TURNS, TURNS):
                next_attr(i)
            sp.wait_ge(s_sums, N_END - 2 + SAME_SLOTS)
            load_attr(TURNS, 0)
            sp.wait_ge(s_tail0, 1)
            full = (END_UNITS[2] - 1) * FEAT
            at = (N_END + 2) * TILES * FEAT
            sp.dma_start(attr_s[1][:, 0:full], attr_main[:, at:at + full]).then_inc(s_tail, 16)
            sp.dma_start(attr_s[1][0:PART_ROWS, full:full + FEAT], attr[FULL_COLS * P:EDGES, :]).then_inc(s_tail, 16)

            for j in FINAL_ORDER:
                uses = 1 + N_END + sum(j < tiles for tiles in END_UNITS) + (2 if j == SUM_TABLE else 0)
                sp.wait_ge(s_table[j], 16 * uses)
                sp.dma_start(partial[:, j * CHUNK_ROW:(j + 1) * CHUNK_ROW],
                             table_v[j][:, 0:CHUNK_ROW]).then_inc(s_part0[j], 16)

            def store_step(g, b):
                sp.wait_ge(s_out, g * 2 + 2)
                for lo, hi in ((0, XPART), (XPART, NP)):
                    sp.dma_start(out_v[lo:hi, bass.ds(g * (2 * DIM), 2 * DIM)],
                                 z[b][lo:hi, :]).then_inc(s_store, 16)
                sp.wait_ge(s_store, g * 32 + 32)
                sp.sem_inc(s_stored, 1)

            sp.sem_inc(s_stored, 2)
            with sp.Fori(0, PAIRS) as m:
                for s in range(PAIR):
                    store_step(m * PAIR + s, s % 2)
            for g in range(PAIRS * PAIR, STEPS):
                store_step(g, g % 2)

        @block.gpsimd
        def _(pool):
            nc.gpsimd.iota(src_i[:, POOL_COLS:POOL_COLS + 1], pattern=[[0, 1]], base=NODES,
                           channel_multiplier=1)
            nc.gpsimd.iota(spare_i[:, :], pattern=[[0, 1]], base=NODES, channel_multiplier=1).then_inc(s_fill, 1)
            pool.sem_inc(s_sent, OUT_SLOTS - 1)
            nc.gpsimd.iota(node_of[:, :].rearrange("p (c n) -> p c n", n=P), pattern=[[1, OH_COLS], [COLS, P]], base=0,
                           channel_multiplier=0).then_inc(s_const, 1)
            nc.gpsimd.memset(eps_col[:, :], EPS).then_inc(s_const, 1)
            nc.gpsimd.memset(ident[:, :], 0.0).then_inc(s_const, 1)
            nc.gpsimd.memset(same_weight[:, :], 1.0).then_inc(s_const, 1)
            pool.wait_ge(s_const, 4)
            nc.gpsimd.affine_select(out=ident[:, :], in_=ident[:, :], compare_op=ALU.not_equal, fill=1.0,
                                    base=0, pattern=[[-1, P]], channel_multiplier=1).then_inc(s_const, 1)
            nc.gpsimd.affine_select(out=same_weight[:, :], in_=same_weight[:, :], compare_op=ALU.is_ge, fill=DUP,
                                    base=0, pattern=[[1, P]], channel_multiplier=-1).then_inc(s_const, 1)
            pool.wait_ge(s_zero, 1)
            for j in range(TILES):
                pool.dma_start(table_v[j].rearrange("p (k w) -> p k w", k=CHUNKS),
                               partial[:, 0:CHUNK_ROW].unsqueeze(1).to_broadcast([P, CHUNKS, CHUNK_ROW])
                               ).then_inc(s_table[j], 16)

            def scatter_unit(n, s, passes, tiles=TILES):
                pool.wait_ge(s_idx, n + (1 + OUT_SLOTS))
                pool.wait_ge(s_pay, n + (1 + SUM_SLOTS))
                for j in range(tiles):
                    extra = passes if j == SUM_TABLE else 0
                    pool.wait_ge(s_table[j], n * 16 + 16 * (1 + extra))
                    pool.sem_inc(s_own, 1)
                    pool.indirect_dma_start(
                        out=tables[j], out_offset=bass.IndirectOffsetOnAxis(ap=idx[s][:, j:j + 1], axis=0),
                        in_=payload[s][:, j, :], in_offset=None, compute_op=ALU.add,
                        engine_sem=s_sent if j == tiles - 1 else None).then_inc(s_table[j], 16)

            def scatter_turns(first, end, passes):
                with pool.Fori(first, end) as i:
                    for s in range(UNITS):
                        scatter_unit(i * UNITS + s, s, passes)

            def add_pass(h, units):
                pool.wait_ge(s_pass_out, (h + 1) * len(direct_p))
                pool.wait_ge(s_table[SUM_TABLE], 16 * (1 + units + h))
                at = h * PASS_COLS * ROW
                pool.dma_start(table_v[SUM_TABLE][:, at:at + PASS_COLS * ROW], direct_sum,
                               accum_op=ALU.add).then_inc(s_table[SUM_TABLE], 16)

            scatter_turns(0, PASS_TURNS, 0)
            add_pass(0, PASS_TURNS * UNITS)
            scatter_turns(PASS_TURNS, 2 * PASS_TURNS, 1)
            for i in range(2 * PASS_TURNS, TURNS):
                for s in range(UNITS):
                    scatter_unit(i * UNITS + s, s, 1)
            add_pass(1, TURNS * UNITS)
            for s, tiles in enumerate(END_UNITS):
                scatter_unit(N_END + s, s, 2, tiles)

            def add_tables(k, b):
                pool.wait_ge(s_aggt_p, k * CHUNK_STEPS + CHUNK_STEPS)
                for j in range(1, TILES):
                    if j > 1:
                        pool.wait_ge(s_acc, (k - 1) * (TILES - 1) + (j - 1))
                    nc.gpsimd.tensor_tensor(acc[b], partial[:, 0:CHUNK_ROW] if j == 1 else acc[b],
                                            partial[:, j * CHUNK_ROW:(j + 1) * CHUNK_ROW],
                                            ALU.add).then_inc(s_acc, 1)

            def load_chunk(k):
                if k > 1:
                    pool.wait_ge(s_acc, (k - 1) * (TILES - 1))
                for j in range(TILES):
                    pool.dma_start(partial[:, j * CHUNK_ROW:(j + 1) * CHUNK_ROW],
                                   table_v[j][:, bass.ds(k * CHUNK_ROW, CHUNK_ROW)]).then_inc(s_part, 16)

            pool.wait_ge(s_acc0, TILES - 1)
            for k in range(1, CHUNKS):
                load_chunk(k)
                pool.wait_ge(s_part, k * (16 * TILES))
                add_tables(k, k % 2)

        @block.scalar
        def _(act):
            act.sem_inc(s_pay, SUM_SLOTS)
            act.sem_inc(s_xt, 1)
            act.wait_ge(s_srcf, 2)

            def stage(n, s, tiles=TILES):
                act.wait_ge(s_idx, n + 1)
                first = n * TILES
                nc.scalar.copy(src_unit[s][:, 0:tiles], srcf[:, bass.ds(first, tiles)]).then_inc(s_staged, 1)

            def evacuate(n, s, tiles=TILES):
                act.wait_ge(s_sums, n + (1 + SAME_SLOTS))
                act.wait_ge(s_idx, n + (1 + OUT_SLOTS))
                nc.scalar.copy(payload[s][:, 0:tiles, 0:FEAT],
                               sums_p[:, 0:tiles * FEAT].rearrange("p (t f) -> p t f", f=FEAT)
                               ).then_inc(s_pay, 1)

            def stage_x(d, q):
                act.wait_ge(s_xb, d + 1)
                act.wait_ge(s_xt_p, d + 1)
                nc.scalar.copy(x_stage[q][0:NP, :], xs[0:NP, bass.ds(d * DIM, DIM)]).then_inc(s_xstage, 1)

            def save_xt(d):
                act.wait_ge(s_xt_p, d + 3)
                act.wait_ge(s_pre_p, d + 1)
                nc.scalar.copy(xt[:, :, :], xt_p.rearrange("p (k n) -> p k n", n=NP)).then_inc(s_xt, 1)

            def high_part(i, g):
                act.wait_ge(s_raw[g], i * 16 + 16)
                act.wait_ge(s_used, i * (2 * DIRECT) + (g + 1) * DIRECT)
                nc.scalar.copy(parts[g][:, :, 0:FEAT], raw[g]).then_inc(s_hi, 1)

            def middle_part(i, g):
                act.wait_ge(s_rest, i * 2 + (g + 1))
                nc.scalar.copy(parts[g][:, :, FEAT + 2:2 * FEAT + 2], raw[g]).then_inc(s_mid, 1)

            def turn(i, d, direct):
                n = i * UNITS
                stage(n + 1, 1)
                if d is not None:
                    stage_x(d, 0)
                if direct:
                    high_part(i, 0)
                    middle_part(i, 0)
                evacuate(n, 0)
                if d is not None:
                    save_xt(d)
                stage(n + 2, 2)
                if direct:
                    high_part(i, 1)
                    middle_part(i, 1)
                evacuate(n + 1, 1)
                stage(n + 3, 3)
                if d is not None:
                    stage_x(d + 1, 1)
                evacuate(n + 2, 2)
                if d is not None:
                    save_xt(d + 1)
                stage(n + 4, 0)
                evacuate(n + 3, 3)

            def save_pass(h):
                act.wait_ge(s_pass, h + 1)
                if h == 1:
                    act.wait_ge(s_table[SUM_TABLE], 16 * (2 + PASS_TURNS * UNITS))
                at = 0
                for bank in direct_p:
                    n = bank.shape[1]
                    nc.scalar.copy(direct_sum[:, at:at + n], bank).then_inc(s_pass_out, 1)
                    at += n

            stage(0, 0)
            with act.Fori(0, PLAIN_TURNS) as i:
                turn(i, None, True)
            act.wait_ge(s_x, 2 * 16 * X_PIECES)
            with act.Fori(PLAIN_TURNS, PASS_TURNS) as i:
                turn(i, i * 2 - 2 * PLAIN_TURNS, True)
            save_pass(0)
            with act.Fori(PASS_TURNS, 2 * PASS_TURNS) as i:
                turn(i, i * 2 - 2 * PLAIN_TURNS, True)
            save_pass(1)
            for i in range(2 * PASS_TURNS, TURNS):
                turn(i, i * 2 - 2 * PLAIN_TURNS, False)
            for s, tiles in enumerate(END_UNITS):
                if s + 1 < len(END_UNITS):
                    stage(N_END + s + 1, s + 1, END_UNITS[s + 1])
                evacuate(N_END + s, s, tiles)

            act.sem_inc(s_aggt, 2)

            def save_aggt(g, b):
                act.wait_ge(s_aggt_p, g + (1 + PAIR))
                act.wait_ge(s_h_p, g + 1)
                nc.scalar.copy(aggt[b][0:FEAT, :], aggt_p[b]).then_inc(s_aggt, 1)

            def relu(g, b):
                act.wait_ge(s_hsum, g * 2 + (2 + 4))
                nc.scalar.activation(h_s[b], h_s[b], ACT.Relu).then_inc(s_h, 1)

            def normalize(g, b):
                act.wait_ge(s_mv, g * 2 + 2)
                nc.scalar.activation(std[0:NP, b, :], mv[0:NP, b, :, 1], ACT.Sqrt,
                                     bias=eps_col[0:NP, :]).then_inc(s_std, 1)
                act.wait_ge(s_shift, g + 1)
                for c in range(2):
                    nc.scalar.activation(z[b][0:NP, c * DIM:(c + 1) * DIM], z[b][0:NP, c * DIM:(c + 1) * DIM],
                                         ACT.Identity, scale=rstd[0:NP, b, c:c + 1],
                                         bias=shift[0:NP, b, c:c + 1]).then_inc(s_out, 1)

            def step(g, b, left=STEPS):
                if left > 2:
                    save_aggt(g + 2, b)
                if left > 1:
                    relu(g + 1, 1 - b)
                normalize(g, b)

            save_aggt(0, 0)
            save_aggt(1, 1)
            relu(0, 0)
            with act.Fori(0, PAIRS) as m:
                for s in range(PAIR):
                    step(m * PAIR + s, s % 2)
            for g in range(PAIRS * PAIR, STEPS):
                step(g, g % 2, STEPS - g)

        @block.tensor
        def _(pe):
            pe.sem_inc(s_sums, SAME_SLOTS)
            pe.sem_inc(s_aggt_p, PAIR)
            pe.sem_inc(s_xt_p, 2)
            pe.sem_inc(s_used, 2 * DIRECT)
            pe.sem_inc(s_pre_p, 1)
            pe.wait_ge(s_const, 6)

            def spread(n, s, tiles=TILES):
                pe.wait_ge(s_staged, n + 1)
                pe.wait_ge(s_same, n + SAME_SLOTS)
                for t in range(tiles):
                    last = nc.tensor.transpose(rows_p[:, t * P:(t + 1) * P],
                                               src_unit[s][:, t:t + 1].to_broadcast([P, P]), ident[:, :])
                last.then_inc(s_rows, 1)

            def add_up(n, s, tiles=TILES):
                pe.wait_ge(s_same, n + (1 + SAME_SLOTS))
                pe.wait_ge(s_pay, n + 1)
                for t in range(tiles):
                    at = (s % 2 * TILES + t) * FEAT
                    last = nc.tensor.matmul(sums_p[:, t * FEAT:(t + 1) * FEAT], same[s % 2][:, t, :],
                                            attr_s[s // 2][:, at:at + FEAT], start=True, stop=True)
                last.then_inc(s_sums, 1)

            def transpose_x(d, q):
                pe.wait_ge(s_xstage, d + 1)
                pe.wait_ge(s_pre, d + 1)
                for k in range(KX):
                    last = nc.tensor.transpose(xt_p[:, k * NP:(k + 1) * NP], x_stage[q][0:NP, k * P:(k + 1) * P],
                                               ident[0:NP, 0:NP])
                last.then_inc(s_xt_p, 1)

            def first_layer_x(d):
                pe.wait_ge(s_xt, d + 2)
                for k in range(KH):
                    for c in range(KX):
                        last = nc.tensor.matmul(pre_p[:, k * NP:(k + 1) * NP], w1x[:, c, k * P:(k + 1) * P],
                                                xt[:, c, :], start=(c == 0), stop=(c == KX - 1))
                last.then_inc(s_pre_p, 1)

            def open_pass():
                for bank in direct_p:
                    nc.tensor.matmul(bank, zeros[:, :], zeros[:, 0:1].to_broadcast([P, bank.shape[1]]),
                                     start=True, stop=False)

            def close_pass():
                for bank in direct_p:
                    last = nc.tensor.matmul(bank, zeros[:, :], zeros[:, 0:1].to_broadcast([P, bank.shape[1]]),
                                            start=False, stop=True)
                last.then_inc(s_pass, 1)

            def direct_tile(i, q):
                g, t = q // 2, q % 2
                pe.wait_ge(s_lo, i * 2 + (g + 1 + 2))
                for h in range(2):
                    first, count = HALVES[h]
                    pe.wait_ge(s_onehot, i * (2 * DIRECT) + (2 * q + h + 1))
                    for c in range(count):
                        bank, at = (first + c) // BANK_COLS, (first + c) % BANK_COLS * ROW
                        nodes = onehot[h][:, c * P:(c + 1) * P]
                        nc.tensor.matmul(direct_p[bank][:, at:at + ROW], nodes, parts[g][:, t, 0:ROW],
                                         start=False, stop=False)
                        for low in range(2):
                            part_at = FEAT + 2 + low * FEAT
                            last = nc.tensor.matmul(direct_p[bank][:, at:at + FEAT], nodes,
                                                    parts[g][:, t, part_at:part_at + FEAT], start=False, stop=False)
                    last.then_inc(s_used, 1)

            def turn(i, d, direct):
                n = i * UNITS
                for s in range(UNITS):
                    if s % 2 == 0:
                        pe.wait_ge(s_attr[s // 2], i * 16 + 16)
                    add_up(n + s, s)
                    spread(n + s + 1, (s + 1) % UNITS)
                    if d is not None and s % 2 == 0:
                        transpose_x(d + s // 2, s // 2)
                    if direct:
                        direct_tile(i, s)
                    if d is not None and s % 2 == 0:
                        first_layer_x(d + s // 2)

            spread(0, 0)
            pe.wait_ge(s_direct, 7)
            open_pass()
            with pe.Fori(0, PLAIN_TURNS) as i:
                turn(i, None, True)
            pe.wait_ge(s_w, 5 * 16)
            for k in range(KH):
                last = nc.tensor.matmul(bias_p[:, k:k + 1], w1u[:, k * P:(k + 1) * P], u_col[:, :],
                                        start=True, stop=True)
            last.then_inc(s_bias_p, 1)
            pe.wait_ge(s_bias, 1)
            with pe.Fori(PLAIN_TURNS, PASS_TURNS) as i:
                turn(i, i * 2 - 2 * PLAIN_TURNS, True)
            close_pass()
            pe.wait_ge(s_pass_out, len(direct_p))
            open_pass()
            with pe.Fori(PASS_TURNS, 2 * PASS_TURNS) as i:
                turn(i, i * 2 - 2 * PLAIN_TURNS, True)
            close_pass()
            for i in range(2 * PASS_TURNS, TURNS):
                turn(i, i * 2 - 2 * PLAIN_TURNS, False)
            for s, tiles in enumerate(END_UNITS):
                if s == 0:
                    pe.wait_ge(s_attr[0], 16 * (TURNS + 1))
                if s == 2:
                    pe.wait_ge(s_tail, 2 * 16)
                add_up(N_END + s, s, tiles)
                if s + 1 < len(END_UNITS):
                    spread(N_END + s + 1, s + 1, END_UNITS[s + 1])

            pe.wait_ge(s_pay, ALL_UNITS + SUM_SLOTS)
            pe.wait_ge(s_pre, COLS + 1)
            pe.wait_ge(s_pass_out, 2 * len(direct_p))
            pe.wait_ge(s_w2, 2 * 16)
            pe.sem_inc(s_h_p, 2)
            pe.sem_inc(s_y, 2)

            def transpose_means(g, b, s):
                pe.wait_ge(s_aggt, g + 1)
                pe.sem_inc(s_own_pe, 1)
                means = acc[s // CHUNK_STEPS % 2].rearrange("p (c r) -> p c r", r=ROW)
                for c in range(2):
                    last = nc.tensor.transpose(aggt_p[b][:, c * NP:(c + 1) * NP],
                                               means[0:NP, s % CHUNK_STEPS * 2 + c, 0:FEAT], ident[0:NP, 0:NP])
                last.then_inc(s_aggt_p, 1)

            def first_layer_edges(g, b):
                pe.wait_ge(s_aggt, g + 3)
                pe.wait_ge(s_hsum, g * 2 + 2)
                for k in range(KH):
                    at = k // 2 * 512 + k % 2 * NW
                    last = nc.tensor.matmul(h_p[b][:, at:at + NW], w1e[:, k * P:(k + 1) * P],
                                            aggt[b][0:FEAT, :], start=True, stop=True)
                last.then_inc(s_h_p, 1)

            def second_layer(g, b):
                pe.wait_ge(s_h, g + 1)
                pe.wait_ge(s_z, g * 2 + 2)
                for c in range(2):
                    for k in range(KH):
                        at = k * NW + c * NP
                        last = nc.tensor.matmul(y_p[b][0:NP, c * DIM:(c + 1) * DIM], h_s[b][:, at:at + NP],
                                                w2s[:, k, :], start=(k == 0), stop=(k == KH - 1))
                last.then_inc(s_y, 1)

            def step(m, s, left=STEPS):
                g = m * PAIR + s
                b = s % 2
                if left > 2:
                    ahead = s + 2
                    if ahead % CHUNK_STEPS == 0:
                        pe.wait_ge(s_agg, m * 2 + (ahead // CHUNK_STEPS + 1))
                    transpose_means(g + 2, b, ahead)
                if left > 1:
                    first_layer_edges(g + 1, 1 - b)
                second_layer(g, b)

            pe.wait_ge(s_agg, 1)
            transpose_means(0, 0, 0)
            transpose_means(1, 1, 1)
            first_layer_edges(0, 0)
            with pe.Fori(0, PAIRS) as m:
                for s in range(PAIR):
                    step(m, s)
            for g in range(PAIRS * PAIR, STEPS):
                step(PAIRS, g - PAIRS * PAIR, STEPS - g)

        @block.vector
        def _(dve):
            dve.sem_inc(s_same, SAME_SLOTS)
            dve.sem_inc(s_idx, OUT_SLOTS)
            dve.sem_inc(s_xb, 2)
            dve.sem_inc(s_pre, 1)
            nc.vector.memset(partial[:, 0:CHUNK_ROW], 0.0).then_inc(s_zero, 1)
            dve.sem_inc(s_lo, 2)
            nc.vector.memset(zeros[:, :], 0.0).then_inc(s_direct, 1)
            for g in range(2):
                nc.vector.memset(parts[g][:, :, FEAT:FEAT + 2], 1.0).then_inc(s_direct, 1)
            dve.wait_ge(s_src, 16 * 3)
            nc.vector.tensor_copy(srcf[:, :], src_i).then_inc(s_srcf, 1)
            nc.vector.tensor_copy(spare_row[:, :], spare_i[:, :]).then_inc(s_srcf, 1)
            dve.wait_ge(s_srcf, 2)
            for h, (first, _) in enumerate(HALVES):
                nc.vector.tensor_scalar(src_direct[:, h, :], srcf[:, POOL_COLS + 1:SRC_COLS], float(-first), None,
                                        ALU.add).then_inc(s_direct, 1)
            dve.wait_ge(s_direct, 7)
            dve.wait_ge(s_const, 6)

            def mark(n, s, tiles=TILES):
                b = s % 2
                ids = src_unit[s][:, 0:tiles]
                dve.wait_ge(s_rows, n + 1)
                dve.wait_ge(s_sums, n + 1)
                nc.vector.tensor_tensor(same[b][:, 0:tiles, :],
                                        rows_p[:, 0:tiles * P].rearrange("p (t e) -> p t e", e=P),
                                        ids.unsqueeze(2).to_broadcast([P, tiles, P]),
                                        ALU.is_equal).then_inc(s_same, 1)
                dve.wait_ge(s_same, n + (1 + SAME_SLOTS))
                nc.vector.tensor_tensor(wsame[:, 0:tiles, :], same[b][:, 0:tiles, :],
                                        same_weight[:, :].unsqueeze(1).to_broadcast([P, tiles, P]),
                                        ALU.mult).then_inc(s_wsame, 1)
                dve.wait_ge(s_wsame, n + 1)
                dve.wait_ge(s_sent, n + 1)
                count = payload[s][:, 0:tiles, FEAT:ROW]
                nc.vector.tensor_reduce(count, wsame[:, 0:tiles, :], AX.X, ALU.add).then_inc(s_weight, 1)
                dve.wait_ge(s_weight, n + 1)
                nc.vector.tensor_scalar(t_dup[:, 0:tiles].unsqueeze(2), count, DUP, spare_row[:, 0:1],
                                        ALU.is_ge, ALU.mult).then_inc(s_dup, 1)
                dve.wait_ge(s_dup, n + 1)
                nc.vector.tensor_tensor(idx[s][:, 0:tiles], t_dup[:, 0:tiles], ids, ALU.max).then_inc(s_idx, 1)

            def add_b2(d, q):
                dve.wait_ge(s_xstage, d + 1)
                nc.vector.tensor_tensor(xs[0:NP, bass.ds(d * DIM, DIM)], x_stage[q][0:NP, :], b2_all[0:NP, :],
                                        ALU.add).then_inc(s_xb, 1)

            def save_pre(d):
                dve.wait_ge(s_pre_p, d + 2)
                nc.vector.tensor_tensor(pre[:, bass.ds(d * (KH * NP), KH * NP)].rearrange("p (k n) -> p k n", n=NP),
                                        pre_p.rearrange("p (k n) -> p k n", n=NP),
                                        hid_bias[:, :].unsqueeze(2).to_broadcast([P, KH, NP]),
                                        ALU.add).then_inc(s_pre, 1)

            def split(i, g):
                dve.wait_ge(s_hi, i * 2 + (g + 1))
                nc.vector.tensor_tensor(raw[g], raw[g], parts[g][:, :, 0:FEAT], ALU.subtract).then_inc(s_rest, 1)
                dve.wait_ge(s_mid, i * 2 + (g + 1))
                nc.vector.tensor_tensor(parts[g][:, :, 2 * FEAT + 2:3 * FEAT + 2], raw[g],
                                        parts[g][:, :, FEAT + 2:2 * FEAT + 2], ALU.subtract).then_inc(s_lo, 1)

            def find_nodes(i, q, first, h0):
                for h in range(2):
                    n = HALVES[h0 + h][1] * P
                    dve.wait_ge(s_used, i * (2 * DIRECT) + (2 * q + h + 2 * DIRECT - 1))
                    nc.vector.tensor_scalar(onehot[h][:, 0:n], node_of[:, 0:n],
                                            src_direct[:, h0 + h, bass.ds(first + q, 1)], None,
                                            ALU.is_equal).then_inc(s_onehot, 1)

            def turn(i, d, first=None, h0=0):
                n = i * UNITS
                for s in range(UNITS):
                    mark(n + s, s)
                    if first is not None:
                        if s < 2:
                            split(i, s)
                        find_nodes(i, s, first, h0)
                    if d is not None:
                        if s % 2 == 0:
                            add_b2(d + s // 2, s // 2)
                        else:
                            save_pre(d + s // 2)

            with dve.Fori(0, PLAIN_TURNS) as i:
                turn(i, None, i * DIRECT)
            dve.wait_ge(s_w, 5 * 16)
            dve.wait_ge(s_bias_p, 1)
            nc.vector.tensor_tensor(hid_bias[:, :], bias_p, b1_col[:, :], ALU.add).then_inc(s_bias, 1)
            dve.wait_ge(s_bias, 1)
            with dve.Fori(PLAIN_TURNS, PASS_TURNS) as i:
                turn(i, i * 2 - 2 * PLAIN_TURNS, i * DIRECT)
            with dve.Fori(PASS_TURNS, 2 * PASS_TURNS) as i:
                turn(i, i * 2 - 2 * PLAIN_TURNS, i * DIRECT - DIRECT_COLS, 2)
            for i in range(2 * PASS_TURNS, TURNS):
                turn(i, i * 2 - 2 * PLAIN_TURNS)
            dve.wait_ge(s_sums, N_END + SAME_SLOTS)
            full = (END_UNITS[2] - 1) * FEAT
            nc.vector.memset(attr_s[1][:, full:full + FEAT], 0.0).then_inc(s_tail0, 1)
            for s, tiles in enumerate(END_UNITS):
                mark(N_END + s, s, tiles)

            dve.sem_inc(s_hsum, 4)
            dve.sem_inc(s_z, 4)

            def part(j):
                return partial[:, j * CHUNK_ROW:(j + 1) * CHUNK_ROW]

            def chunk_means(k, b):
                rows = acc[b].rearrange("p (c r) -> p c r", r=ROW)
                nc.vector.tensor_scalar(rcount[:, :].unsqueeze(2), rows[:, :, FEAT:ROW], 1.0, None,
                                        ALU.max).then_inc(s_rc, 1)
                dve.wait_ge(s_rc, k * 2 + 1)
                nc.vector.reciprocal(rcount[:, :], rcount[:, :]).then_inc(s_rc, 1)
                dve.wait_ge(s_rc, k * 2 + 2)
                nc.vector.tensor_tensor(rows[:, :, 0:FEAT], rows[:, :, 0:FEAT],
                                        rcount[:, :].unsqueeze(2).to_broadcast([P, CC, FEAT]),
                                        ALU.mult).then_inc(s_agg, 1)

            def hidden_sum(g, b):
                dve.wait_ge(s_h_p, g + 3)
                dve.wait_ge(s_y, g + 1)
                both = pre[:, bass.ds(g * (2 * KH * NP), 2 * KH * NP)].rearrange("p (c k n) -> p k c n", c=2, n=NP)
                for r in range(2):
                    nc.vector.tensor_tensor(
                        h_s[b][:, r * 2 * NW:(r + 1) * 2 * NW].rearrange("p (k c n) -> p k c n", k=2, c=2),
                        h_p[b][:, r * 512:r * 512 + 2 * NW].rearrange("p (k c n) -> p k c n", k=2, c=2),
                        both[:, 2 * r:2 * r + 2, :, :], ALU.add).then_inc(s_hsum, 1)

            def layer_norm(g, b):
                dve.wait_ge(s_y, g + 3)
                dve.wait_ge(s_stored, g + 1)
                for c in range(2):
                    nc.vector.tensor_tensor(z[b][0:NP, c * DIM:(c + 1) * DIM], y_p[b][0:NP, c * DIM:(c + 1) * DIM],
                                            xs[0:NP, bass.ds(g * (2 * DIM) + c * DIM, DIM)],
                                            ALU.add).then_inc(s_z, 1)
                dve.wait_ge(s_z, g * 2 + (2 + 4))
                for c in range(2):
                    nc.vector.bn_stats(stats[0:NP, b, c, :], z[b][0:NP, c * DIM:(c + 1) * DIM]).then_inc(s_stats, 1)
                dve.wait_ge(s_stats, g * 2 + 2)
                dve.sem_inc(s_own_dve, 1)
                for c in range(2):
                    nc.vector.bn_aggr(mv[0:NP, b, c, :], stats[0:NP, b, c, :]).then_inc(s_mv, 1)
                dve.wait_ge(s_std, g + 1)
                nc.vector.reciprocal(rstd[0:NP, b, :], std[0:NP, b, :]).then_inc(s_rstd, 1)
                dve.wait_ge(s_rstd, g + 1)
                nc.vector.scalar_tensor_tensor(shift[0:NP, b, :], mv[0:NP, b, :, 0], -1.0, rstd[0:NP, b, :],
                                               ALU.mult, ALU.mult).then_inc(s_shift, 1)

            def step(m, s, left=STEPS):
                g = m * PAIR + s
                if left > 1:
                    hidden_sum(g + 1, (s + 1) % 2)
                if s % CHUNK_STEPS == 1 and left > CHUNK_STEPS:
                    k = s // CHUNK_STEPS + 1
                    dve.wait_ge(s_acc, (m * 2 + k) * (TILES - 1))
                    chunk_means(m * 2 + k, k % 2)
                layer_norm(g, s % 2)

            a, b, *others = FINAL_ORDER
            dve.wait_ge(s_part0[a], 16)
            dve.wait_ge(s_part0[b], 16)
            nc.vector.tensor_tensor(acc[0], part(a), part(b), ALU.add).then_inc(s_acc0, 1)
            for n, j in enumerate(others):
                dve.wait_ge(s_part0[j], 16)
                dve.wait_ge(s_acc0, n + 1)
                nc.vector.tensor_tensor(acc[0], acc[0], part(j), ALU.add).then_inc(s_acc0, 1)
            dve.wait_ge(s_acc0, TILES - 1)
            chunk_means(0, 0)
            hidden_sum(0, 0)
            with dve.Fori(0, PAIRS) as m:
                for s in range(PAIR):
                    step(m, s)
            for g in range(PAIRS * PAIR, STEPS):
                step(PAIRS, g - PAIRS * PAIR, STEPS - g)


_INS = ["x", "src", "edge_attr_64", "L0_gnn_u", "L0_gnn_W1", "L0_gnn_b1", "L0_gnn_W2", "L0_gnn_b2"]


def kernel(**inputs):
    import numpy as _np
    import concourse.bacc as _bacc
    from concourse import mybir as _mybir
    from concourse.bass_utils import run_bass_kernel_spmd as _run

    nc = _bacc.Bacc("TRN2", target_bir_lowering=False, num_devices=1)
    arrays, args = {}, []
    for name in _INS:
        a = _np.ascontiguousarray(inputs[name])
        arrays[f"in_{name}"] = a
        args.append(nc.dram_tensor(f"in_{name}", a.shape, _mybir.dt.from_np(a.dtype), kind="ExternalInput").ap())
    out = nc.dram_tensor("out_0", (NODES, DIM), F32, kind="ExternalOutput").ap()
    build(nc, *args, out)
    r = _run(nc, [arrays], core_ids=[0])
    return r.results[0]["out_0"]
```

```python
from contextlib import ExitStack

import concourse.bass as bass
from concourse import mybir

F32 = mybir.dt.float32
F32R = mybir.dt.float32r
BF16 = mybir.dt.bfloat16
I16 = mybir.dt.int16
I32 = mybir.dt.int32
U32 = mybir.dt.uint32
ALU = mybir.AluOpType
ACT = mybir.ActivationFunctionType
AX = mybir.AxisListType

P = 128
NODES, DIM = 6250, 256
EDGES, FEAT = 100000, 64
HID = 512
EPS = 1e-5

ROW = FEAT + 1
TILES = 5
UNITS = 4
FULL_COLS = EDGES // P
PART_ROWS = EDGES - FULL_COLS * P
PASS_TURNS = 17
TURNS = 2 * PASS_TURNS
GROUPS = [(0, 3), (3, 2)]
DIRECT = sum(count for _, count in GROUPS)
DIRECT_AT = [(0,), (1, 2), (3,), (4,)]
DIRECT_COLS = PASS_TURNS * DIRECT
POOL_COLS = FULL_COLS - DIRECT_COLS
N_END = TURNS * UNITS
END_COLS = POOL_COLS - N_END * TILES
END_UNITS = [TILES, TILES, TILES, END_COLS + 1 - 3 * TILES]
assert 0 < END_UNITS[3] <= TILES and len(END_UNITS) == UNITS and PART_ROWS > 0
ALL_UNITS = N_END + len(END_UNITS)
END_TILES = sum(END_UNITS[2:])
SRC_COLS = FULL_COLS + 1
FINAL_ORDER = [*range(END_UNITS[3], TILES), *range(END_UNITS[3])]
EARLY = 3
LATE_PIECES = [(0, 3), (3, 2)]
LATE_FROM = UNITS - 1
FIRST_TABLES = [[(s * TILES + j) % EARLY if s < LATE_FROM else j for j in range(TILES)] for s in range(UNITS)]
ZERO_DMAS = [int(j < EARLY) for j in range(TILES)]
BEFORE = [ZERO_DMAS[j] + sum(tiles.count(j) for tiles in FIRST_TABLES) - UNITS for j in range(TILES)]
SUM_TABLE = TILES - 1
HALVES = [(0, 13), (13, 12), (25, 13), (38, 12)]
OH_COLS = 13
BANK_COLS = 512 // ROW
DUP = 256.0

NP = 125
COLS = NODES // NP
TABLE_ROWS = P * COLS
XPART = 112
KX = DIM // P
KH = HID // P
PASS_COLS = COLS // 2
DENSE_TURNS = COLS // 2
PLAIN_TURNS = TURNS - DENSE_TURNS
X_PIECES = 8
X_PIECE = COLS * DIM // X_PIECES
assert X_PIECES <= PLAIN_TURNS
CHUNKS = 5
CC = COLS // CHUNKS
CHUNK_STEPS = CC // 2
STEPS = COLS // 2
PAIR = 2 * CHUNK_STEPS
PAIRS = STEPS // PAIR
CHUNK_ROW = CC * ROW
NW = 2 * NP
ADD_STEPS = [-1, 0, 0, 1]
LOAD_AT = [1, CHUNK_STEPS, 2 * CHUNK_STEPS]

SAME_SLOTS = 2
SUM_SLOTS = 1
OUT_SLOTS = 4


def build(nc, x, src, attr, u, w1, b1, w2, b2, out):
    tables = [nc.dram_tensor(f"table{j}", [TABLE_ROWS, ROW], F32, kind="Internal").ap()
              for j in range(TILES)]
    src_main = src[0:FULL_COLS * P].rearrange("(p t) -> p t", p=P)
    attr_main = attr[0:FULL_COLS * P, :].rearrange("(p t) f -> p (t f)", p=P)
    x_v = x.rearrange("(p c) d -> p (c d)", p=NP)
    out_v = out.rearrange("(p c) d -> p (c d)", p=NP)
    table_v = [t.rearrange("(p c) r -> p (c r)", p=P) for t in tables]

    ctx = ExitStack()
    edge_ctx = ExitStack()
    with ctx:
        def sb(name, shape, dt=F32):
            return ctx.enter_context(nc.sbuf_tensor(name, shape, dt))

        def edge_sb(name, shape, dt=F32):
            return edge_ctx.enter_context(nc.sbuf_tensor(name, shape, dt))

        def pb(name, shape, dt=F32):
            return ctx.enter_context(nc.psum_tensor(name, shape, dt))

        def sem(name):
            return ctx.enter_context(nc.semaphore(name))

        ident = sb("ident", [P, P])
        spare_row = sb("spare_row", [P, 1])
        spare_i = sb("spare_i", [P, 1], I32)
        b2_all = sb("b2_all", [P, DIM])
        b1_col = sb("b1_col", [P, KH])
        u_col = sb("u_col", [P, 1])
        hid_bias = sb("hid_bias", [P, KH])

        xs = sb("xs", [P, COLS * DIM])
        pre = sb("pre", [P, COLS * HID // P * NP])
        partial = sb("partial", [P, TILES * CHUNK_ROW])
        rcount = sb("rcount", [P, CC])
        stats = sb("stats", [P, 2, 2, 6])
        mv = sb("mv", [P, 2, 2, 2])
        std = sb("std", [P, 2, 2])
        rstd = sb("rstd", [P, 2, 2])
        shift = sb("shift", [P, 2, 2])
        eps_col = sb("eps_col", [P, 1])

        acc = [sb("acc0", [P, CHUNK_ROW])[:, :], None]

        same_weight = edge_sb("same_weight", [P, P])
        w1x = edge_sb("w1x", [P, KX, HID])
        xt = edge_sb("xt", [P, KX, NP])
        srcf = edge_sb("srcf", [P, SRC_COLS])
        src_parts = edge_sb("src_parts", [P, 2, POOL_COLS + 1], BF16)
        parts_unit = [edge_sb(f"parts_unit{s}", [P, 2, TILES], BF16) for s in range(UNITS)]
        src_unit = [edge_sb(f"src_unit{s}", [P, TILES]) for s in range(UNITS)]
        t_dup = edge_sb("t_dup", [P, TILES])
        zeros = edge_sb("zeros", [P, P], BF16)[:, :]
        ident_b = edge_sb("ident_b", [P, P], BF16)[:, :]
        HALF = 2 * TILES
        PART_LEN = 3 * FEAT + 2
        attr_raw = [edge_sb(f"attr_raw{a}", [P, HALF, FEAT])[:, :, :] for a in range(2)]
        attr_parts = [edge_sb(f"attr_parts{a}", [P, HALF, PART_LEN], BF16) for a in range(2)]
        same = [edge_sb(f"same{b}", [P, TILES, P], BF16) for b in range(2)]
        raw = [acc[0][:, q * FEAT:(q + count) * FEAT].rearrange("p (t f) -> p t f", f=FEAT) for q, count in GROUPS]
        parts = [edge_sb(f"parts{g}", [P, count, PART_LEN], BF16) for g, (_, count) in enumerate(GROUPS)]
        node_of = edge_sb("node_of", [P, OH_COLS * P], I16)
        src_direct = edge_sb("src_direct", [P, len(HALVES), DIRECT_COLS])
        x_stage = [edge_sb("x_stage0", [P, DIM])[:, :], acc[0][:, DIRECT * FEAT:DIRECT * FEAT + DIM]]
        assert DIRECT * FEAT + DIM <= CHUNK_ROW
        payload = [edge_sb(f"payload{s}", [P, TILES, ROW]) for s in range(UNITS)]
        idx = [edge_sb(f"idx{s}", [P, TILES], U32) for s in range(UNITS)]
        edge_ctx.close()
        src_i = pre[:, 0:SRC_COLS].bitcast(I32)
        w1u = pre[:, 1024:1024 + HID]
        direct_sum = partial[:, 0:PASS_COLS * ROW]
        onehot = [partial[:, at:at + cols * P // 2].bitcast(BF16)
                  for at, cols in ((PASS_COLS * ROW, HALVES[0][1]),
                                   (PASS_COLS * ROW + HALVES[0][1] * P // 2, HALVES[1][1]))]
        assert PASS_COLS * (ROW + P // 2) <= TILES * CHUNK_ROW

        z_both = sb("z", [P, 2 * 2 * DIM])
        z = [z_both[:, b * 2 * DIM:(b + 1) * 2 * DIM] for b in range(2)]
        w2_raw = z_both[:, :]
        w1e_raw = acc[0][0:FEAT, 0:HID]
        w2r = [sb(f"w2_{part}", [P, KH * DIM], F32R) for part in ("high", "low")]
        w1er = [sb(f"w1e_{part}", [FEAT, HID], F32R) for part in ("high", "low")]
        aggt = [[sb(f"aggt{b}_{part}", [FEAT, NW], F32R) for part in ("high", "low")] for b in range(2)]
        acc[1] = sb("acc1", [P, CHUNK_ROW])[:, :]
        h_r = [[sb(f"h{b}_{part}", [P, KH * NW], F32R) for part in ("high", "low")] for b in range(2)]

        ps = pb("ps", [P, 8 * 512])
        rows_p = ps[:, 0:TILES * P]
        sums_p = ps[:, 2 * 512:2 * 512 + TILES * ROW]
        bias_p = ps[:, 3 * 512:3 * 512 + KH]
        xt_p = ps[:, 3 * 512:3 * 512 + KX * NP]
        pre_p = ps[:, 3 * 512:3 * 512 + KH * NP]
        direct_p = [ps[:, (4 + g) * 512:(4 + g) * 512 + min(BANK_COLS, PASS_COLS - g * BANK_COLS) * ROW]
                    for g in range(-(-PASS_COLS // BANK_COLS))]
        h_p = [ps[:, 2 * b * 512:(2 * b + 2) * 512] for b in range(2)]
        y_p = [ps[:, (4 + b) * 512:(5 + b) * 512] for b in range(2)]
        aggt_p = [ps[0:FEAT, (6 + b) * 512:(6 + b) * 512 + NW] for b in range(2)]

        s_fill = sem("s_fill")
        s_src = sem("s_src")
        s_srcf = sem("s_srcf")
        s_const = sem("s_const")
        s_zero = sem("s_zero")
        s_table = [sem(f"s_table{j}") for j in range(TILES)]
        s_late = [sem(f"s_late{j}") for j in range(EARLY, TILES)]
        s_attr = [sem(f"s_attr{a}") for a in range(2)]
        s_attr_hi = sem("s_attr_hi")
        s_attr_rest = sem("s_attr_rest")
        s_attr_mid = sem("s_attr_mid")
        s_attr_lo = sem("s_attr_lo")
        s_tail0 = sem("s_tail0")
        s_tail = sem("s_tail")
        s_raw = [sem(f"s_raw{g}") for g in range(2)]
        s_hi = sem("s_hi")
        s_rest = sem("s_rest")
        s_mid = sem("s_mid")
        s_lo = sem("s_lo")
        s_direct = sem("s_direct")
        s_onehot = sem("s_onehot")
        s_used = sem("s_used")
        s_pass = sem("s_pass")
        s_pass_out = sem("s_pass_out")
        s_w = sem("s_w")
        s_w2 = sem("s_w2")
        s_bias_p = sem("s_bias_p")
        s_bias = sem("s_bias")
        s_x = sem("s_x")
        s_staged = sem("s_staged")
        s_rows = sem("s_rows")
        s_same = sem("s_same")
        s_sums = sem("s_sums")
        s_dup = sem("s_dup")
        s_idx = sem("s_idx")
        s_pay = sem("s_pay")
        s_sent = sem("s_sent")
        s_xstage = sem("s_xstage")
        s_xb = sem("s_xb")
        s_xt_p = sem("s_xt_p")
        s_xt = sem("s_xt")
        s_pre_p = sem("s_pre_p")
        s_pre = sem("s_pre")
        s_own = sem("s_own")
        s_own_dve = sem("s_own_dve")
        s_own_pe = sem("s_own_pe")
        s_own_act = sem("s_own_act")
        s_part0 = [sem(f"s_part0_{j}") for j in range(TILES)]
        s_acc0 = sem("s_acc0")
        s_part = sem("s_part")
        s_acc = sem("s_acc")
        s_rc = sem("s_rc")
        s_agg = sem("s_agg")
        s_aggt_p = sem("s_aggt_p")
        s_aggt = sem("s_aggt")
        s_aggt_lo = sem("s_aggt_lo")
        s_h_p = sem("s_h_p")
        s_hsum = sem("s_hsum")
        s_h = sem("s_h")
        s_relu = sem("s_relu")
        s_h_lo = sem("s_h_lo")
        s_w_hi = sem("s_w_hi")
        s_w_lo = sem("s_w_lo")
        s_y = sem("s_y")
        s_z = sem("s_z")
        s_stats = sem("s_stats")
        s_mv = sem("s_mv")
        s_std = sem("s_std")
        s_rstd = sem("s_rstd")
        s_shift = sem("s_shift")
        s_out = sem("s_out")
        s_store = [sem(f"s_store{b}") for b in range(2)]

        block = ctx.enter_context(nc.Block())

        @block.sync
        def _(sp):
            sp.wait_ge(s_fill, 1)
            with nc.allow_non_contiguous_dma(reason="one edge per partition"):
                sp.dma_start(src_i[:, 0:POOL_COLS], src_main[:, 0:POOL_COLS]).then_inc(s_src, 16)
                sp.dma_start(src_i[:, POOL_COLS + 1:SRC_COLS], src_main[:, POOL_COLS:FULL_COLS]).then_inc(s_src, 16)
                sp.dma_start(src_i[0:PART_ROWS, POOL_COLS:POOL_COLS + 1],
                             src[FULL_COLS * P:EDGES].rearrange("(p o) -> p o", o=1)).then_inc(s_src, 16)

            def load_attr(k, a):
                sp.dma_start(attr_raw[a].rearrange("p t f -> p (t f)"),
                             attr_main[:, bass.ds(k * (HALF * FEAT), HALF * FEAT)]).then_inc(s_attr[a], 16)

            def load_raw(i, g, first):
                q, count = GROUPS[g]
                sp.wait_ge(s_lo, i * 2 + (g + 1))
                sp.dma_start(raw[g].rearrange("p t f -> p (t f)"),
                             attr_main[:, bass.ds(first * FEAT + (POOL_COLS + q) * FEAT, count * FEAT)]
                             ).then_inc(s_raw[g], 16)

            load_attr(0, 0)
            load_raw(0, 0, 0)
            load_raw(0, 1, 0)
            load_attr(1, 1)

            def zero_table(j):
                for n, (first, count) in enumerate(LATE_PIECES):
                    if n > 0:
                        sp.wait_ge(s_late[j - EARLY], 16 * n)
                    sp.dma_start(table_v[j].rearrange("p (k w) -> p k w", k=CHUNKS)[:, first:first + count, :],
                                 partial[:, 0:CHUNK_ROW].unsqueeze(1).to_broadcast([P, count, CHUNK_ROW])
                                 ).then_inc(s_late[j - EARLY], 16)

            for j in range(EARLY):
                sp.wait_ge(s_table[j], 16)
            zero_table(EARLY)
            load_raw(1, 0, DIRECT)
            sp.wait_ge(s_attr_lo, 1)
            load_attr(2, 0)
            zero_table(EARLY + 1)
            load_raw(1, 1, DIRECT)
            sp.wait_ge(s_attr_lo, 2)
            load_attr(3, 1)
            sp.dma_start(w1x[:, :, :], w1[0:DIM, :].rearrange("(k p) n -> p k n", p=P)).then_inc(s_w, 16)
            sp.dma_start(w1u, w1[DIM + FEAT:DIM + FEAT + P, :]).then_inc(s_w, 16)
            with nc.allow_non_contiguous_dma(reason="a vector down the partitions"):
                sp.dma_start(u_col[:, :], u[0, :].rearrange("(p o) -> p o", o=1)).then_inc(s_w, 16)
                sp.dma_start(b1_col[:, :], b1.rearrange("(k p) -> p k", p=P)).then_inc(s_w, 16)
            sp.dma_start(b2_all[:, :], b2.partition_broadcast(P)).then_inc(s_w, 16)

            def turn(i, first):
                if first is not None:
                    load_raw(i + 1, 0, first)
                sp.wait_ge(s_attr_lo, i * 2 + 1)
                load_attr(i * 2 + 2, 0)
                if first is not None:
                    load_raw(i + 1, 1, first)
                    sp.wait_ge(s_attr_lo, i * 2 + 2)
                    load_attr(i * 2 + 3, 1)

            def load_x(i):
                for lo, hi in ((0, XPART), (XPART, NP)):
                    sp.dma_start(xs[lo:hi, bass.ds(i * X_PIECE, X_PIECE)],
                                 x_v[lo:hi, bass.ds(i * X_PIECE, X_PIECE)]).then_inc(s_x, 16)

            load_x(0)
            with sp.Fori(1, X_PIECES) as i:
                turn(i, i * DIRECT + DIRECT)
                load_x(i)
            with sp.Fori(X_PIECES, PASS_TURNS - 1) as i:
                turn(i, i * DIRECT + DIRECT)
            with sp.Fori(PASS_TURNS - 1, TURNS - 1) as i:
                turn(i, i * DIRECT + DIRECT - DIRECT_COLS)
            turn(TURNS - 1, None)
            sp.wait_ge(s_tail0, 1)
            full = (END_TILES - 1) * FEAT
            at = (N_END + 2) * TILES * FEAT
            tail = attr_raw[1].rearrange("p t f -> p (t f)")
            sp.dma_start(tail[:, 0:full], attr_main[:, at:at + full]).then_inc(s_tail, 16)
            sp.dma_start(tail[0:PART_ROWS, full:full + FEAT], attr[FULL_COLS * P:EDGES, :]).then_inc(s_tail, 16)
            sp.wait_ge(s_idx, ALL_UNITS + OUT_SLOTS)
            sp.dma_start(w1e_raw, w1[DIM:DIM + FEAT, :]).then_inc(s_w2, 16)
            sp.dma_start(w2_raw.rearrange("p (k n) -> p k n", n=DIM), w2.rearrange("(k p) n -> p k n", p=P)
                         ).then_inc(s_w2, 16)

            for j in FINAL_ORDER:
                uses = BEFORE[j] + N_END + sum(j < tiles for tiles in END_UNITS) + (2 if j == SUM_TABLE else 0)
                sp.wait_ge(s_table[j], 16 * uses)
                sp.dma_start(partial[:, j * CHUNK_ROW:(j + 1) * CHUNK_ROW],
                             table_v[j][:, 0:CHUNK_ROW]).then_inc(s_part0[j], 16)

            def store_step(g, b):
                sp.wait_ge(s_out, g * 2 + 2)
                for lo, hi in ((0, XPART), (XPART, NP)):
                    sp.dma_start(out_v[lo:hi, bass.ds(g * (2 * DIM), 2 * DIM)],
                                 z[b][lo:hi, :]).then_inc(s_store[b], 16)

            def load_chunk(k):
                if k == 1:
                    sp.wait_ge(s_acc0, TILES - 1)
                else:
                    sp.wait_ge(s_acc, (k - 1) * (TILES - 1))
                for j in range(TILES):
                    sp.dma_start(partial[:, j * CHUNK_ROW:(j + 1) * CHUNK_ROW],
                                 table_v[j][:, k * CHUNK_ROW:(k + 1) * CHUNK_ROW]).then_inc(s_part, 16)

            load_chunk(1)
            for g in range(STEPS):
                if g in LOAD_AT:
                    load_chunk(2 + LOAD_AT.index(g))
                store_step(g, g % 2)
            sp.wait_ge(s_store[0], 32 * ((STEPS + 1) // 2 + 1))
            sp.wait_ge(s_store[1], 32 * (STEPS // 2 + 1))

        @block.gpsimd
        def _(pool):
            nc.gpsimd.iota(src_i[:, POOL_COLS:POOL_COLS + 1], pattern=[[0, 1]], base=NODES,
                           channel_multiplier=1)
            nc.gpsimd.iota(spare_i[:, :], pattern=[[0, 1]], base=NODES, channel_multiplier=1).then_inc(s_fill, 1)
            pool.sem_inc(s_sent, OUT_SLOTS - 1)
            nc.gpsimd.iota(node_of[:, :].rearrange("p (c n) -> p c n", n=P), pattern=[[1, OH_COLS], [COLS, P]], base=0,
                           channel_multiplier=0).then_inc(s_const, 1)
            nc.gpsimd.memset(eps_col[:, :], EPS).then_inc(s_const, 1)
            nc.gpsimd.memset(ident[:, :], 0.0).then_inc(s_const, 1)
            nc.gpsimd.memset(same_weight[:, :], 1.0).then_inc(s_const, 1)
            pool.wait_ge(s_const, 4)
            nc.gpsimd.affine_select(out=ident[:, :], in_=ident[:, :], compare_op=ALU.not_equal, fill=1.0,
                                    base=0, pattern=[[-1, P]], channel_multiplier=1).then_inc(s_const, 1)
            nc.gpsimd.affine_select(out=same_weight[:, :], in_=same_weight[:, :], compare_op=ALU.is_ge, fill=DUP,
                                    base=0, pattern=[[-1, P]], channel_multiplier=1).then_inc(s_const, 1)
            pool.wait_ge(s_zero, 1)
            for j in range(EARLY):
                pool.dma_start(table_v[j].rearrange("p (k w) -> p k w", k=CHUNKS),
                               partial[:, 0:CHUNK_ROW].unsqueeze(1).to_broadcast([P, CHUNKS, CHUNK_ROW])
                               ).then_inc(s_table[j], 16)

            def scatter(s, t, j, last):
                pool.sem_inc(s_own, 1)
                pool.indirect_dma_start(
                    out=tables[j], out_offset=bass.IndirectOffsetOnAxis(ap=idx[s][:, t:t + 1], axis=0),
                    in_=payload[s][:, t, :], in_offset=None, compute_op=ALU.add,
                    engine_sem=s_sent if last else None).then_inc(s_table[j], 16)

            def scatter_unit(n, s, passes, tiles=TILES):
                pool.wait_ge(s_idx, n + (1 + OUT_SLOTS))
                for j in range(tiles):
                    extra = passes if j == SUM_TABLE else 0
                    pool.wait_ge(s_table[j], n * 16 + 16 * (BEFORE[j] + extra))
                    scatter(s, j, j, j == tiles - 1)

            done = list(ZERO_DMAS)
            for s in range(UNITS):
                pool.wait_ge(s_idx, s + (1 + OUT_SLOTS))
                for t, j in enumerate(FIRST_TABLES[s]):
                    if done[j] > 0:
                        pool.wait_ge(s_table[j], 16 * done[j])
                    else:
                        pool.wait_ge(s_late[j - EARLY], 16 * len(LATE_PIECES))
                    scatter(s, t, j, t == TILES - 1)
                    done[j] += 1

            def scatter_turns(first, end, passes):
                with pool.Fori(first, end) as i:
                    for s in range(UNITS):
                        scatter_unit(i * UNITS + s, s, passes)

            def add_pass(h, units):
                pool.wait_ge(s_pass_out, (h + 1) * len(direct_p))
                pool.wait_ge(s_table[SUM_TABLE], 16 * (BEFORE[SUM_TABLE] + units + h))
                at = h * PASS_COLS * ROW
                pool.dma_start(table_v[SUM_TABLE][:, at:at + PASS_COLS * ROW], direct_sum,
                               accum_op=ALU.add).then_inc(s_table[SUM_TABLE], 16)

            scatter_turns(1, PASS_TURNS, 0)
            add_pass(0, PASS_TURNS * UNITS)
            scatter_turns(PASS_TURNS, 2 * PASS_TURNS, 1)
            add_pass(1, TURNS * UNITS)
            for s, tiles in enumerate(END_UNITS):
                scatter_unit(N_END + s, s, 2, tiles)

            def add_table(k, j):
                if j == 1:
                    pool.wait_ge(s_part, k * (16 * TILES))
                    pool.wait_ge(s_aggt_p, k * CHUNK_STEPS + CHUNK_STEPS)
                else:
                    pool.wait_ge(s_acc, (k - 1) * (TILES - 1) + (j - 1))
                nc.gpsimd.tensor_tensor(acc[k % 2], partial[:, 0:CHUNK_ROW] if j == 1 else acc[k % 2],
                                        partial[:, j * CHUNK_ROW:(j + 1) * CHUNK_ROW], ALU.add).then_inc(s_acc, 1)

            def low_hidden(g, b):
                for c in range(2):
                    at, end = c * KH * NP, (c + 1) * KH * NP
                    pool.wait_ge(s_relu, g * 2 + c + 1)
                    nc.gpsimd.tensor_tensor(h_r[b][1][:, at:end], pre[:, g * KH * NW + at:g * KH * NW + end],
                                            h_r[b][0][:, at:end].bitcast(F32), ALU.subtract).then_inc(s_h_lo, 1)

            pool.sem_inc(s_h_lo, 4)
            additions = {0: [(1, 1)], 1: [(1, 2)], 2: [(1, 3), (1, 4)]}
            for k in range(2, CHUNKS):
                for g, j in zip(ADD_STEPS, range(1, TILES)):
                    additions.setdefault((k - 1) * CHUNK_STEPS + g, []).append((k, j))
            for g in range(STEPS):
                for k, j in additions.get(g, []):
                    add_table(k, j)
                low_hidden(g, g % 2)

        @block.scalar
        def _(act):
            act.sem_inc(s_pay, SUM_SLOTS)
            act.sem_inc(s_xt, 1)
            act.wait_ge(s_srcf, 4)

            def stage(n, s, tiles=TILES):
                act.wait_ge(s_idx, n + 1)
                first = n * TILES
                nc.scalar.copy(src_unit[s][:, 0:tiles], srcf[:, bass.ds(first, tiles)]).then_inc(s_staged, 1)
                nc.scalar.copy(parts_unit[s][:, :, 0:tiles], src_parts[:, :, bass.ds(first, tiles)]).then_inc(s_staged, 1)

            def evacuate(n, s, tiles=TILES):
                act.wait_ge(s_sent, n + 1)
                act.wait_ge(s_sums, n + (1 + SAME_SLOTS))
                nc.scalar.copy(payload[s][:, 0:tiles, :], sums_p[:, 0:tiles * ROW].rearrange("p (t r) -> p t r", r=ROW)
                               ).then_inc(s_pay, 1)

            def stage_x(d, q):
                act.wait_ge(s_xb, d + 1)
                act.wait_ge(s_xt_p, d + 1)
                nc.scalar.copy(x_stage[q][0:NP, :], xs[0:NP, bass.ds(d * DIM, DIM)]).then_inc(s_xstage, 1)

            def save_xt(d):
                act.wait_ge(s_xt_p, d + 3)
                act.wait_ge(s_pre_p, d + 1)
                nc.scalar.copy(xt[:, :, :], xt_p.rearrange("p (k n) -> p k n", n=NP)).then_inc(s_xt, 1)

            def attr_high(k, a, loaded, tiles=HALF, first=False):
                if tiles == HALF:
                    act.wait_ge(s_attr[a], loaded * 16)
                else:
                    act.wait_ge(s_tail, 2 * 16)
                if not first:
                    act.wait_ge(s_sums, k * 2)
                nc.scalar.copy(attr_parts[a][:, 0:tiles, 0:FEAT], attr_raw[a][:, 0:tiles, :]).then_inc(s_attr_hi, 1)

            def attr_middle(k, a, tiles=HALF):
                act.wait_ge(s_attr_rest, k + 1)
                nc.scalar.copy(attr_parts[a][:, 0:tiles, FEAT + 2:2 * FEAT + 2],
                               attr_raw[a][:, 0:tiles, :]).then_inc(s_attr_mid, 1)

            def high_part(i, g, used):
                act.wait_ge(s_raw[g], i * 16 + 16)
                act.wait_ge(s_used, used)
                nc.scalar.copy(parts[g][:, :, 0:FEAT], raw[g]).then_inc(s_hi, 1)

            def middle_part(i, g):
                act.wait_ge(s_rest, i * 2 + (g + 1))
                nc.scalar.copy(parts[g][:, :, FEAT + 2:2 * FEAT + 2], raw[g]).then_inc(s_mid, 1)

            def turn(i, d, last=False):
                n = i * UNITS
                stage(n + 1, 1)
                if d is not None:
                    stage_x(d, 0)
                attr_high(i * 2 + 1, 1, i + 1)
                high_part(i, 1, i * (2 * DIRECT) + 2 * DIRECT)
                evacuate(n, 0)
                if d is not None:
                    save_xt(d)
                stage(n + 2, 2)
                attr_middle(i * 2 + 1, 1)
                middle_part(i, 1)
                evacuate(n + 1, 1)
                stage(n + 3, 3)
                if d is not None:
                    stage_x(d + 1, 1)
                attr_high(i * 2 + 2, 0, i + 2)
                if not last:
                    high_part(i + 1, 0, i * (2 * DIRECT) + 2 * (DIRECT + GROUPS[0][1]))
                evacuate(n + 2, 2)
                if d is not None:
                    save_xt(d + 1)
                stage(n + 4, 0)
                attr_middle(i * 2 + 2, 0)
                if not last:
                    middle_part(i + 1, 0)
                evacuate(n + 3, 3)

            def save_pass(h):
                act.wait_ge(s_pass, h + 1)
                if h == 1:
                    act.wait_ge(s_table[SUM_TABLE], 16 * (BEFORE[SUM_TABLE] + PASS_TURNS * UNITS + 1))
                at = 0
                for bank in direct_p:
                    n = bank.shape[1]
                    nc.scalar.copy(direct_sum[:, at:at + n], bank).then_inc(s_pass_out, 1)
                    at += n

            stage(0, 0)
            attr_high(0, 0, 1, first=True)
            high_part(0, 0, 2 * DIRECT)
            attr_middle(0, 0)
            middle_part(0, 0)
            with act.Fori(0, PLAIN_TURNS) as i:
                turn(i, None)
            act.wait_ge(s_x, 2 * 16 * X_PIECES)
            with act.Fori(PLAIN_TURNS, PASS_TURNS) as i:
                turn(i, i * 2 - 2 * PLAIN_TURNS)
            save_pass(0)
            with act.Fori(PASS_TURNS, TURNS - 1) as i:
                turn(i, i * 2 - 2 * PLAIN_TURNS)
            turn(TURNS - 1, COLS - 2, last=True)
            save_pass(1)
            for s, tiles in enumerate(END_UNITS):
                if s + 1 < len(END_UNITS):
                    stage(N_END + s + 1, s + 1, END_UNITS[s + 1])
                if s == 0:
                    attr_high(2 * TURNS + 1, 1, TURNS + 1, END_TILES)
                    attr_middle(2 * TURNS + 1, 1, END_TILES)
                evacuate(N_END + s, s, tiles)

            act.wait_ge(s_w2, 2 * 16)
            nc.scalar.copy(w1er[0][:, :], w1e_raw).then_inc(s_w_hi, 1)
            nc.scalar.copy(w2r[0][:, :], w2_raw).then_inc(s_w_hi, 1)

            def save_aggt(g, b):
                act.wait_ge(s_aggt_p, g + (1 + PAIR))
                act.wait_ge(s_h_p, g + 1)
                nc.scalar.copy(aggt[b][0][:, :], aggt_p[b]).then_inc(s_aggt, 1)

            def relu(g, b):
                act.wait_ge(s_hsum, g * 2 + (2 + 4))
                act.wait_ge(s_y, g + 1)
                act.sem_inc(s_own_act, 1)
                nc.scalar.activation(h_r[b][0][:, :], pre[:, bass.ds(g * (KH * NW), KH * NW)], ACT.Relu).then_inc(s_h, 1)
                act.wait_ge(s_h, g + 1)
                act.sem_inc(s_own_act, 1)
                for c in range(2):
                    column = pre[:, bass.ds(g * (KH * NW) + c * (KH * NP), KH * NP)]
                    nc.scalar.activation(column, column, ACT.Relu).then_inc(s_relu, 1)

            def deviation(g, b):
                act.wait_ge(s_mv, g * 2 + 2)
                nc.scalar.activation(std[0:NP, b, :], mv[0:NP, b, :, 1], ACT.Sqrt,
                                     bias=eps_col[0:NP, :]).then_inc(s_std, 1)

            def normalize(g, b):
                act.wait_ge(s_shift, g + 1)
                for c in range(2):
                    nc.scalar.activation(z[b][0:NP, c * DIM:(c + 1) * DIM], z[b][0:NP, c * DIM:(c + 1) * DIM],
                                         ACT.Identity, scale=rstd[0:NP, b, c:c + 1],
                                         bias=shift[0:NP, b, c:c + 1]).then_inc(s_out, 1)

            def step(g, b, left=STEPS):
                deviation(g, b)
                if left > 3:
                    save_aggt(g + 3, 1 - b)
                if left > 2:
                    relu(g + 2, b)
                normalize(g, b)

            save_aggt(0, 0)
            save_aggt(1, 1)
            relu(0, 0)
            save_aggt(2, 0)
            relu(1, 1)
            with act.Fori(0, PAIRS) as m:
                for s in range(PAIR):
                    step(m * PAIR + s, s % 2)
            for g in range(PAIRS * PAIR, STEPS):
                step(g, g % 2, STEPS - g)

        @block.tensor
        def _(pe):
            pe.sem_inc(s_sums, SAME_SLOTS)
            pe.sem_inc(s_aggt_p, PAIR)
            pe.sem_inc(s_xt_p, 2)
            pe.sem_inc(s_used, 2 * DIRECT)
            pe.sem_inc(s_pre_p, 1)
            pe.wait_ge(s_const, 6)

            def spread(n, s, tiles=TILES):
                pe.wait_ge(s_staged, n * 2 + 2)
                pe.wait_ge(s_same, n + SAME_SLOTS)
                for t in range(tiles):
                    for part in range(2):
                        last = nc.tensor.matmul(rows_p[:, t * P:(t + 1) * P],
                                                parts_unit[s][:, part, t:t + 1].to_broadcast([P, P]), ident_b,
                                                start=(part == 0), stop=(part == 1))
                last.then_inc(s_rows, 1)

            def add_up(n, s, half, tiles=TILES):
                pe.wait_ge(s_same, n + (1 + SAME_SLOTS))
                pe.wait_ge(s_pay, n + 1)
                if s % 2 == 0:
                    pe.wait_ge(s_attr_lo, half + 1)
                for t in range(tiles):
                    edges = same[s % 2][:, t, :]
                    row = attr_parts[s // 2][:, s % 2 * TILES + t, :]
                    nc.tensor.matmul(sums_p[:, t * ROW:(t + 1) * ROW], edges, row[:, 0:ROW], start=True, stop=False)
                    for low in range(2):
                        part_at = FEAT + 2 + low * FEAT
                        last = nc.tensor.matmul(sums_p[:, t * ROW:t * ROW + FEAT], edges,
                                                row[:, part_at:part_at + FEAT], start=False, stop=(low == 1))
                last.then_inc(s_sums, 1)

            def transpose_x(d, q):
                pe.wait_ge(s_xstage, d + 1)
                pe.wait_ge(s_pre, d + 1)
                for k in range(KX):
                    last = nc.tensor.transpose(xt_p[:, k * NP:(k + 1) * NP], x_stage[q][0:NP, k * P:(k + 1) * P],
                                               ident[0:NP, 0:NP])
                last.then_inc(s_xt_p, 1)

            def first_layer_x(d):
                pe.wait_ge(s_xt, d + 2)
                for k in range(KH):
                    for c in range(KX):
                        last = nc.tensor.matmul(pre_p[:, k * NP:(k + 1) * NP], w1x[:, c, k * P:(k + 1) * P],
                                                xt[:, c, :], start=(c == 0), stop=(c == KX - 1))
                last.then_inc(s_pre_p, 1)

            def open_pass():
                for bank in direct_p:
                    nc.tensor.matmul(bank, zeros, zeros[:, 0:1].to_broadcast([P, bank.shape[1]]),
                                     start=True, stop=False)

            def close_pass():
                for bank in direct_p:
                    last = nc.tensor.matmul(bank, zeros, zeros[:, 0:1].to_broadcast([P, bank.shape[1]]),
                                            start=False, stop=True)
                last.then_inc(s_pass, 1)

            def direct_tile(i, q):
                g = int(q >= GROUPS[1][0])
                t = q - GROUPS[g][0]
                pe.wait_ge(s_lo, i * 2 + (g + 1 + 2))
                for h in range(2):
                    first, count = HALVES[h]
                    pe.wait_ge(s_onehot, i * (2 * DIRECT) + (2 * q + h + 1))
                    for c in range(count):
                        bank, at = (first + c) // BANK_COLS, (first + c) % BANK_COLS * ROW
                        nodes = onehot[h][:, c * P:(c + 1) * P]
                        nc.tensor.matmul(direct_p[bank][:, at:at + ROW], nodes, parts[g][:, t, 0:ROW],
                                         start=False, stop=False)
                        for low in range(2):
                            part_at = FEAT + 2 + low * FEAT
                            last = nc.tensor.matmul(direct_p[bank][:, at:at + FEAT], nodes,
                                                    parts[g][:, t, part_at:part_at + FEAT], start=False, stop=False)
                    last.then_inc(s_used, 1)

            def turn(i, d):
                n = i * UNITS
                for s in range(UNITS):
                    add_up(n + s, s, i * 2 + s // 2)
                    spread(n + s + 1, (s + 1) % UNITS)
                    if d is not None and s % 2 == 0:
                        transpose_x(d + s // 2, s // 2)
                    for q in DIRECT_AT[s]:
                        direct_tile(i, q)
                    if d is not None and s % 2 == 0:
                        first_layer_x(d + s // 2)

            pe.wait_ge(s_direct, 10)
            spread(0, 0)
            open_pass()
            with pe.Fori(0, PLAIN_TURNS) as i:
                turn(i, None)
            pe.wait_ge(s_w, 5 * 16)
            for k in range(KH):
                last = nc.tensor.matmul(bias_p[:, k:k + 1], w1u[:, k * P:(k + 1) * P], u_col[:, :],
                                        start=True, stop=True)
            last.then_inc(s_bias_p, 1)
            pe.wait_ge(s_bias, 1)
            with pe.Fori(PLAIN_TURNS, PASS_TURNS) as i:
                turn(i, i * 2 - 2 * PLAIN_TURNS)
            close_pass()
            pe.wait_ge(s_pass_out, len(direct_p))
            open_pass()
            with pe.Fori(PASS_TURNS, 2 * PASS_TURNS) as i:
                turn(i, i * 2 - 2 * PLAIN_TURNS)
            close_pass()
            for s, tiles in enumerate(END_UNITS):
                add_up(N_END + s, s, 2 * TURNS + s // 2, tiles)
                if s + 1 < len(END_UNITS):
                    spread(N_END + s + 1, s + 1, END_UNITS[s + 1])

            pe.wait_ge(s_pay, ALL_UNITS + SUM_SLOTS)
            pe.wait_ge(s_pre, COLS + 1)
            pe.wait_ge(s_pass_out, 2 * len(direct_p))
            pe.wait_ge(s_w_lo, 2)
            pe.sem_inc(s_h_p, 2)
            pe.sem_inc(s_y, 2)

            def transpose_means(g, b, s):
                pe.wait_ge(s_aggt_lo, g + 1)
                pe.sem_inc(s_own_pe, 1)
                means = acc[s // CHUNK_STEPS % 2].rearrange("p (c r) -> p c r", r=ROW)
                for c in range(2):
                    last = nc.tensor.transpose(aggt_p[b][:, c * NP:(c + 1) * NP],
                                               means[0:NP, s % CHUNK_STEPS * 2 + c, 0:FEAT], ident[0:NP, 0:NP])
                last.then_inc(s_aggt_p, 1)

            def first_layer_edges(g, b):
                pe.wait_ge(s_aggt_lo, g + 3)
                pe.wait_ge(s_hsum, g * 2 + 2)
                for k in range(KH):
                    at = k // 2 * 512 + k % 2 * NW
                    for w_part, part in ((0, 0), (1, 0), (0, 1)):
                        last = nc.tensor.matmul(h_p[b][:, at:at + NW], w1er[w_part][:, k * P:(k + 1) * P],
                                                aggt[b][part][:, :], start=(w_part == part == 0), stop=(part == 1))
                last.then_inc(s_h_p, 1)

            def second_layer(g, b):
                pe.wait_ge(s_h, g + 1)
                pe.wait_ge(s_z, g * 2 + 2)
                for c in range(2):
                    for part in range(2):
                        if part == 1:
                            pe.wait_ge(s_h_lo, g * 2 + (c + 1 + 4))
                        for k in range(KH):
                            at = (c * KH + k) * NP
                            for w_part in range(2 - part):
                                last = nc.tensor.matmul(y_p[b][0:NP, c * DIM:(c + 1) * DIM],
                                                        h_r[b][part][:, at:at + NP],
                                                        w2r[w_part][:, k * DIM:(k + 1) * DIM],
                                                        start=(part == k == w_part == 0), stop=(part == 1 and k == KH - 1))
                last.then_inc(s_y, 1)

            def step(m, s, left=STEPS):
                g = m * PAIR + s
                b = s % 2
                if left > 2:
                    ahead = s + 2
                    if ahead % CHUNK_STEPS == 0:
                        pe.wait_ge(s_agg, m * 2 + (ahead // CHUNK_STEPS + 1))
                    transpose_means(g + 2, b, ahead)
                if left > 1:
                    first_layer_edges(g + 1, 1 - b)
                second_layer(g, b)

            pe.wait_ge(s_agg, 1)
            transpose_means(0, 0, 0)
            transpose_means(1, 1, 1)
            first_layer_edges(0, 0)
            with pe.Fori(0, PAIRS) as m:
                for s in range(PAIR):
                    step(m, s)
            for g in range(PAIRS * PAIR, STEPS):
                step(PAIRS, g - PAIRS * PAIR, STEPS - g)

        @block.vector
        def _(dve):
            dve.sem_inc(s_same, SAME_SLOTS)
            dve.sem_inc(s_idx, OUT_SLOTS)
            dve.sem_inc(s_xb, 2)
            dve.sem_inc(s_pre, 1)
            nc.vector.memset(partial[:, 0:CHUNK_ROW], 0.0).then_inc(s_zero, 1)
            dve.sem_inc(s_lo, 2)
            nc.vector.memset(zeros, 0.0).then_inc(s_direct, 1)
            for g in range(2):
                nc.vector.memset(parts[g][:, :, FEAT:FEAT + 2], 1.0).then_inc(s_direct, 1)
                nc.vector.memset(attr_parts[g][:, :, FEAT:FEAT + 2], 1.0).then_inc(s_direct, 1)
            dve.wait_ge(s_src, 16 * 3)
            nc.vector.tensor_copy(srcf[:, :], src_i).then_inc(s_srcf, 1)
            nc.vector.tensor_copy(spare_row[:, :], spare_i[:, :]).then_inc(s_srcf, 1)
            nc.vector.tensor_copy(src_parts[:, 0, :], src_i[:, 0:POOL_COLS + 1]).then_inc(s_srcf, 1)
            dve.wait_ge(s_srcf, 3)
            nc.vector.tensor_tensor(src_parts[:, 1, :], srcf[:, 0:POOL_COLS + 1], src_parts[:, 0, :],
                                    ALU.subtract).then_inc(s_srcf, 1)
            for h, (first, _) in enumerate(HALVES):
                nc.vector.tensor_scalar(src_direct[:, h, :], srcf[:, POOL_COLS + 1:SRC_COLS], float(-first), None,
                                        ALU.add).then_inc(s_direct, 1)
            dve.wait_ge(s_direct, 9)
            dve.wait_ge(s_const, 6)
            nc.vector.tensor_copy(ident_b, ident[:, :]).then_inc(s_direct, 1)

            def weigh(n, s, tiles=TILES):
                b = s % 2
                dve.wait_ge(s_rows, n + 1)
                dve.wait_ge(s_sums, n + 1)
                for t in range(tiles):
                    last = nc.vector.scalar_tensor_tensor(same[b][:, t, :], rows_p[:, t * P:(t + 1) * P],
                                                          src_unit[s][:, t:t + 1], same_weight[:, :],
                                                          ALU.is_equal, ALU.mult)
                last.then_inc(s_same, 1)

            def choose_rows(n, s, tiles=TILES):
                dve.wait_ge(s_pay, n + (1 + SUM_SLOTS))
                nc.vector.tensor_scalar(t_dup[:, 0:tiles].unsqueeze(2), payload[s][:, 0:tiles, FEAT:ROW], DUP,
                                        spare_row[:, 0:1], ALU.is_ge, ALU.mult).then_inc(s_dup, 1)
                dve.wait_ge(s_dup, n + 1)
                nc.vector.tensor_tensor(idx[s][:, 0:tiles], t_dup[:, 0:tiles], src_unit[s][:, 0:tiles],
                                        ALU.max).then_inc(s_idx, 1)

            def add_b2(d, q):
                dve.wait_ge(s_xstage, d + 1)
                nc.vector.tensor_tensor(xs[0:NP, bass.ds(d * DIM, DIM)], x_stage[q][0:NP, :], b2_all[0:NP, :],
                                        ALU.add).then_inc(s_xb, 1)

            def save_pre(d):
                dve.wait_ge(s_pre_p, d + 2)
                nc.vector.tensor_tensor(pre[:, bass.ds(d * (KH * NP), KH * NP)].rearrange("p (k n) -> p k n", n=NP),
                                        pre_p.rearrange("p (k n) -> p k n", n=NP),
                                        hid_bias[:, :].unsqueeze(2).to_broadcast([P, KH, NP]),
                                        ALU.add).then_inc(s_pre, 1)

            def attr_rest(k, a, tiles=HALF):
                dve.wait_ge(s_attr_hi, k + 1)
                nc.vector.tensor_tensor(attr_raw[a][:, 0:tiles, :], attr_raw[a][:, 0:tiles, :],
                                        attr_parts[a][:, 0:tiles, 0:FEAT], ALU.subtract).then_inc(s_attr_rest, 1)

            def attr_low(k, a, tiles=HALF):
                dve.wait_ge(s_attr_mid, k + 1)
                nc.vector.tensor_tensor(attr_parts[a][:, 0:tiles, 2 * FEAT + 2:PART_LEN], attr_raw[a][:, 0:tiles, :],
                                        attr_parts[a][:, 0:tiles, FEAT + 2:2 * FEAT + 2],
                                        ALU.subtract).then_inc(s_attr_lo, 1)

            def rest(i, g):
                dve.wait_ge(s_hi, i * 2 + (g + 1))
                nc.vector.tensor_tensor(raw[g], raw[g], parts[g][:, :, 0:FEAT], ALU.subtract).then_inc(s_rest, 1)

            def low_part(i, g):
                dve.wait_ge(s_mid, i * 2 + (g + 1))
                nc.vector.tensor_tensor(parts[g][:, :, 2 * FEAT + 2:3 * FEAT + 2], raw[g],
                                        parts[g][:, :, FEAT + 2:2 * FEAT + 2], ALU.subtract).then_inc(s_lo, 1)

            def find_nodes(i, q, first, h0):
                for h in range(2):
                    n = HALVES[h0 + h][1] * P
                    dve.wait_ge(s_used, i * (2 * DIRECT) + (2 * q + h + 2 * DIRECT - 1))
                    nc.vector.tensor_scalar(onehot[h][:, 0:n], node_of[:, 0:n],
                                            src_direct[:, h0 + h, bass.ds(first + q, 1)], None,
                                            ALU.is_equal).then_inc(s_onehot, 1)

            def turn(i, d, first, h0=0, last=False):
                n = i * UNITS
                for s in range(UNITS):
                    weigh(n + s, s)
                    find_nodes(i, DIRECT_AT[s][0], first, h0)
                    k, a = i * 2 + (s // 2 + 1), 1 - s // 2
                    m, g = (i, 1) if s < 2 else (i + 1, 0)
                    (attr_low if s % 2 else attr_rest)(k, a)
                    if g or not last:
                        (low_part if s % 2 else rest)(m, g)
                    if d is not None and s % 2 == 0:
                        add_b2(d + s // 2, s // 2)
                    for q in DIRECT_AT[s][1:]:
                        find_nodes(i, q, first, h0)
                    if d is not None and s % 2 == 1:
                        save_pre(d + s // 2)
                    choose_rows(n + s, s)

            attr_rest(0, 0)
            rest(0, 0)
            attr_low(0, 0)
            low_part(0, 0)
            with dve.Fori(0, PLAIN_TURNS) as i:
                turn(i, None, i * DIRECT)
            dve.wait_ge(s_w, 5 * 16)
            dve.wait_ge(s_bias_p, 1)
            nc.vector.tensor_tensor(hid_bias[:, :], bias_p, b1_col[:, :], ALU.add).then_inc(s_bias, 1)
            dve.wait_ge(s_bias, 1)
            with dve.Fori(PLAIN_TURNS, PASS_TURNS) as i:
                turn(i, i * 2 - 2 * PLAIN_TURNS, i * DIRECT)
            with dve.Fori(PASS_TURNS, TURNS - 1) as i:
                turn(i, i * 2 - 2 * PLAIN_TURNS, i * DIRECT - DIRECT_COLS, 2)
            turn(TURNS - 1, COLS - 2, DIRECT_COLS - DIRECT, 2, last=True)
            dve.wait_ge(s_attr_lo, 2 * TURNS)
            nc.vector.memset(attr_raw[1][:, END_TILES - 1, :], 0.0).then_inc(s_tail0, 1)
            for s, tiles in enumerate(END_UNITS):
                weigh(N_END + s, s, tiles)
                if s == 0:
                    attr_rest(2 * TURNS + 1, 1, END_TILES)
                    attr_low(2 * TURNS + 1, 1, END_TILES)
                choose_rows(N_END + s, s, tiles)

            dve.sem_inc(s_hsum, 4)
            dve.sem_inc(s_z, 4)
            dve.sem_inc(s_aggt_lo, 2)
            for b in range(2):
                dve.sem_inc(s_store[b], 32)
            for n, (low, whole, high) in enumerate(((w1er[1], w1e_raw, w1er[0]), (w2r[1], w2_raw, w2r[0]))):
                dve.wait_ge(s_w_hi, n + 1)
                nc.vector.tensor_tensor(low[:, :], whole, high[:, :].bitcast(F32), ALU.subtract).then_inc(s_w_lo, 1)

            def part(j):
                return partial[:, j * CHUNK_ROW:(j + 1) * CHUNK_ROW]

            def chunk_means(k, b):
                rows = acc[b].rearrange("p (c r) -> p c r", r=ROW)
                nc.vector.tensor_scalar(rcount[:, :].unsqueeze(2), rows[:, :, FEAT:ROW], 1.0, None,
                                        ALU.max).then_inc(s_rc, 1)
                dve.wait_ge(s_rc, k * 2 + 1)
                nc.vector.reciprocal(rcount[:, :], rcount[:, :]).then_inc(s_rc, 1)
                dve.wait_ge(s_rc, k * 2 + 2)
                nc.vector.tensor_tensor(rows[:, :, 0:FEAT], rows[:, :, 0:FEAT],
                                        rcount[:, :].unsqueeze(2).to_broadcast([P, CC, FEAT]),
                                        ALU.mult).then_inc(s_agg, 1)

            def hidden_sum(g, b):
                dve.wait_ge(s_h_p, g + 3)
                both = pre[:, bass.ds(g * (2 * KH * NP), 2 * KH * NP)].rearrange("p (c k n) -> p k c n", c=2, n=NP)
                for r in range(2):
                    nc.vector.tensor_tensor(
                        both[:, 2 * r:2 * r + 2, :, :],
                        h_p[b][:, r * 512:r * 512 + 2 * NW].rearrange("p (k c n) -> p k c n", k=2, c=2),
                        both[:, 2 * r:2 * r + 2, :, :], ALU.add).then_inc(s_hsum, 1)

            def low_means(g, b):
                dve.wait_ge(s_aggt, g + 1)
                nc.vector.tensor_tensor(aggt[b][1][:, :], aggt_p[b], aggt[b][0][:, :].bitcast(F32),
                                        ALU.subtract).then_inc(s_aggt_lo, 1)

            def moments(g, b, before):
                dve.wait_ge(s_y, g + 3)
                dve.wait_ge(s_store[b], before * 16 + 32)
                for c in range(2):
                    nc.vector.tensor_tensor(z[b][0:NP, c * DIM:(c + 1) * DIM], y_p[b][0:NP, c * DIM:(c + 1) * DIM],
                                            xs[0:NP, bass.ds(g * (2 * DIM) + c * DIM, DIM)],
                                            ALU.add).then_inc(s_z, 1)
                dve.wait_ge(s_z, g * 2 + (2 + 4))
                for c in range(2):
                    nc.vector.bn_stats(stats[0:NP, b, c, :], z[b][0:NP, c * DIM:(c + 1) * DIM]).then_inc(s_stats, 1)
                dve.wait_ge(s_stats, g * 2 + 2)
                dve.sem_inc(s_own_dve, 1)
                for c in range(2):
                    nc.vector.bn_aggr(mv[0:NP, b, c, :], stats[0:NP, b, c, :]).then_inc(s_mv, 1)

            def finish_norm(g, b):
                dve.wait_ge(s_std, g + 1)
                nc.vector.reciprocal(rstd[0:NP, b, :], std[0:NP, b, :]).then_inc(s_rstd, 1)
                dve.wait_ge(s_rstd, g + 1)
                nc.vector.scalar_tensor_tensor(shift[0:NP, b, :], mv[0:NP, b, :, 0], -1.0, rstd[0:NP, b, :],
                                               ALU.mult, ALU.mult).then_inc(s_shift, 1)

            def step(m, s, left=STEPS):
                g = m * PAIR + s
                moments(g, s % 2, m * PAIR + s // 2 * 2)
                if left > 2:
                    hidden_sum(g + 2, s % 2)
                if s % CHUNK_STEPS == 1 and left > CHUNK_STEPS:
                    k = s // CHUNK_STEPS + 1
                    dve.wait_ge(s_acc, (m * 2 + k) * (TILES - 1))
                    chunk_means(m * 2 + k, k % 2)
                if left > 3:
                    low_means(g + 3, 1 - s % 2)
                finish_norm(g, s % 2)

            dve.wait_ge(s_w_lo, 2)
            a, b, *others = FINAL_ORDER
            dve.wait_ge(s_part0[a], 16)
            dve.wait_ge(s_part0[b], 16)
            nc.vector.tensor_tensor(acc[0], part(a), part(b), ALU.add).then_inc(s_acc0, 1)
            for n, j in enumerate(others):
                dve.wait_ge(s_part0[j], 16)
                dve.wait_ge(s_acc0, n + 1)
                nc.vector.tensor_tensor(acc[0], acc[0], part(j), ALU.add).then_inc(s_acc0, 1)
            dve.wait_ge(s_acc0, TILES - 1)
            chunk_means(0, 0)
            low_means(0, 0)
            low_means(1, 1)
            hidden_sum(0, 0)
            hidden_sum(1, 1)
            low_means(2, 0)
            with dve.Fori(0, PAIRS) as m:
                for s in range(PAIR):
                    step(m, s)
            for g in range(PAIRS * PAIR, STEPS):
                step(PAIRS, g - PAIRS * PAIR, STEPS - g)


_INS = ["x", "src", "edge_attr_64", "L0_gnn_u", "L0_gnn_W1", "L0_gnn_b1", "L0_gnn_W2", "L0_gnn_b2"]


def kernel(**inputs):
    import numpy as _np
    import concourse.bacc as _bacc
    from concourse import mybir as _mybir
    from concourse.bass_utils import run_bass_kernel_spmd as _run

    nc = _bacc.Bacc("TRN2", target_bir_lowering=False, num_devices=1)
    arrays, args = {}, []
    for name in _INS:
        a = _np.ascontiguousarray(inputs[name])
        arrays[f"in_{name}"] = a
        args.append(nc.dram_tensor(f"in_{name}", a.shape, _mybir.dt.from_np(a.dtype), kind="ExternalInput").ap())
    out = nc.dram_tensor("out_0", (NODES, DIM), F32, kind="ExternalOutput").ap()
    build(nc, *args, out)
    r = _run(nc, [arrays], core_ids=[0])
    return r.results[0]["out_0"]
```
